# Optimizing a Trainium2 kernel written in Bass

```python
import numpy as np
import jax
import jax.numpy as jnp

def _softmax(x, axis=-1):
    return jax.nn.softmax(x, axis=axis)

def _gelu(x):
    return jax.nn.gelu(x, approximate=True)

def _silu(x):
    return jax.nn.silu(x)

def _sigmoid(x):
    return jax.nn.sigmoid(x)

def _layernorm(x, axis=-1, eps=1e-05):
    m = jnp.mean(x, axis=axis, keepdims=True)
    v = jnp.var(x, axis=axis, keepdims=True)
    return (x - m) / jnp.sqrt(v + eps)

def _scatter_add(tgt, idx, src, axis=0):
    return tgt.at[idx].add(src)

def _segment_sum(src, seg, n):
    return jax.ops.segment_sum(src, seg, n)
kernel_name = 'mk_cond_seq_d2_seqx_r8_49dce4'

def setup_inputs(seed: int=0):
    np.random.seed(seed)
    _w = jnp.asarray

    def _rec_inputs():
        import jax
        import jax.numpy as jnp
        _rk = jax.random.key(seed)
        x = -0.0002928 + 1 * jax.random.normal(jax.random.fold_in(_rk, 1), (32, 32, 128), jnp.float32)
        _lenS = 32 - jax.random.randint(jax.random.fold_in(_rk, 7), (32,), 0, max(1, 32 // 4) + 1, jnp.int32)
        _lenS2 = 32 - jax.random.randint(jax.random.fold_in(_rk, 8), (32,), 0, max(1, 32 // 4) + 1, jnp.int32)
        cond_2048 = 0.0061147 + 1.02565 * jax.random.normal(jax.random.fold_in(_rk, 11), (32, 256), jnp.float32)
        _validS = jnp.arange(32)[None, :] < _lenS[:, None]
        _validS2 = jnp.arange(32)[None, :] < _lenS2[:, None]
        _causal = jnp.tril(jnp.ones((32, 32), dtype=bool))
        mask_BxS_ik0 = jnp.where(jnp.broadcast_to(_validS[:, :], (32, 32)), 0, 1).astype(jnp.int32)
        return (x, cond_2048, mask_BxS_ik0)
    x, cond_2048, mask_BxS_ik0 = _rec_inputs()

    def _L0_cond_setup():
        import jax, jax.numpy as jnp
        import numpy as np
        D = 128
        DI = 256
        N = 16
        DT_RANK = 64
        D_CONV = 4
        EPS = 1e-05

        def _layernorm(x, g, b):
            mu = jnp.mean(x, axis=-1, keepdims=True)
            var = jnp.mean((x - mu) ** 2, axis=-1, keepdims=True)
            return (x - mu) * jax.lax.rsqrt(var + EPS) * g + b

        def _mamba(xn, in_proj_w, conv_w, conv_b, x_proj_w, dt_proj_w, dt_proj_b, A_log, D_param, out_proj_w):
            b, sl, _ = xn.shape
            xz = jnp.einsum('bsd,ed->bse', xn, in_proj_w)
            x_in, z = jnp.split(xz, 2, axis=-1)
            xt = jnp.transpose(x_in, (0, 2, 1))
            u = jax.lax.conv_general_dilated(xt, conv_w[:, None, :], (1,), [(D_CONV - 1, 0)], feature_group_count=DI, dimension_numbers=('NCH', 'OIH', 'NCH')) + conv_b[None, :, None]
            u = jax.nn.silu(jnp.transpose(u, (0, 2, 1)))
            x_dbl = jnp.einsum('bsd,ed->bse', u, x_proj_w)
            dt_r, B, C = jnp.split(x_dbl, [DT_RANK, DT_RANK + N], axis=-1)
            dt = jax.nn.softplus(jnp.einsum('bsr,dr->bsd', dt_r, dt_proj_w) + dt_proj_b)
            A = -jnp.exp(A_log)

            def step(h, inp):
                dt_t, B_t, C_t, u_t = inp
                dA = jnp.exp(dt_t[:, :, None] * A)
                h = h * dA + (dt_t * u_t)[:, :, None] * B_t[:, None, :]
                y = jnp.einsum('bdn,bn->bd', h, C_t)
                return (h, y)
            seq = (jnp.transpose(dt, (1, 0, 2)), jnp.transpose(B, (1, 0, 2)), jnp.transpose(C, (1, 0, 2)), jnp.transpose(u, (1, 0, 2)))
            h0 = jnp.zeros((b, DI, N), xn.dtype)
            _, ys = jax.lax.scan(step, h0, seq)
            y = jnp.transpose(ys, (1, 0, 2)) + u * D_param
            y = y * jax.nn.silu(z)
            return jnp.einsum('bsd,ed->bse', y, out_proj_w)
        key = jax.random.key(seed)
        ks = jax.random.split(key, 16)
        s = lambda fan: 1.0 / np.sqrt(fan)
        inp = {'x': jax.random.normal(ks[0], (2, 256, D), jnp.float32), 'c': jax.random.normal(ks[1], (2, 2 * D), jnp.float32), 'ln_g': jnp.ones((D,), jnp.float32), 'ln_b': jnp.zeros((D,), jnp.float32), 'ada_w': jax.random.normal(ks[2], (3 * D, 2 * D), jnp.float32) * s(2 * D), 'ada_b': jnp.zeros((3 * D,), jnp.float32), 'in_proj_w': jax.random.normal(ks[3], (2 * DI, D), jnp.float32) * s(D), 'conv_w': jax.random.normal(ks[4], (DI, D_CONV), jnp.float32) * s(D_CONV), 'conv_b': jnp.zeros((DI,), jnp.float32), 'x_proj_w': jax.random.normal(ks[5], (DT_RANK + 2 * N, DI), jnp.float32) * s(DI), 'dt_proj_w': jax.random.normal(ks[6], (DI, DT_RANK), jnp.float32) * s(DT_RANK), 'dt_proj_b': jax.random.uniform(ks[7], (DI,), jnp.float32, -4.0, -2.0), 'A_log': jnp.tile(jnp.log(jnp.arange(1, N + 1, dtype=jnp.float32)), (DI, 1)), 'D_param': jnp.ones((DI,), jnp.float32), 'out_proj_w': jax.random.normal(ks[8], (D, DI), jnp.float32) * s(DI)}
        return inp
    _L0_cond_all = _L0_cond_setup()
    _L0_cond_in = {k: v for k, v in _L0_cond_all.items() if k in ('ln_g', 'ln_b', 'ada_w', 'ada_b', 'in_proj_w', 'conv_w', 'conv_b', 'x_proj_w', 'dt_proj_w', 'dt_proj_b', 'A_log', 'D_param', 'out_proj_w')}
    del _L0_cond_all

    def _L1_cond_setup():
        import jax, jax.numpy as jnp
        import numpy as np
        H = 16
        LN_EPS = 1e-05

        def _layernorm(x, scale, bias):
            mu = jnp.mean(x, axis=-1, keepdims=True)
            var = jnp.var(x, axis=-1, keepdims=True)
            return (x - mu) * jax.lax.rsqrt(var + LN_EPS) * scale + bias
        key = jax.random.key(seed)
        ks = jax.random.split(key, 8)
        B, T, D, E = (4, 512, 128, 256)
        s = 0.02
        return {'x': jax.random.normal(ks[0], (B, T, D), jnp.float32), 'emb': jax.random.normal(ks[1], (B, E), jnp.float32), 'src_mask': jax.random.randint(ks[2], (B, T), 0, 2).astype(jnp.int32), 'norm_scale': jnp.ones((D,), jnp.float32), 'norm_bias': jnp.zeros((D,), jnp.float32), 'Wq': jax.random.normal(ks[3], (D, D), jnp.float32) * s, 'bq': jnp.zeros((D,), jnp.float32), 'Wk': jax.random.normal(ks[4], (D, D), jnp.float32) * s, 'bk': jnp.zeros((D,), jnp.float32), 'Wv': jax.random.normal(ks[5], (D, D), jnp.float32) * s, 'bv': jnp.zeros((D,), jnp.float32), 'film_emb_W': jax.random.normal(ks[6], (E, 2 * D), jnp.float32) * s, 'film_emb_b': jnp.zeros((2 * D,), jnp.float32), 'film_norm_scale': jnp.ones((D,), jnp.float32), 'film_norm_bias': jnp.zeros((D,), jnp.float32), 'film_out_W': jax.random.normal(ks[7], (D, D), jnp.float32) * s, 'film_out_b': jnp.zeros((D,), jnp.float32)}
    _L1_cond_all = _L1_cond_setup()
    _L1_cond_in = {k: v for k, v in _L1_cond_all.items() if k in ('norm_scale', 'norm_bias', 'Wq', 'bq', 'Wk', 'bk', 'Wv', 'bv', 'film_emb_W', 'film_emb_b', 'film_norm_scale', 'film_norm_bias', 'film_out_W', 'film_out_b')}
    del _L1_cond_all
    return {'x': x, 'cond_2048': cond_2048, 'mask_BxS_ik0': mask_BxS_ik0, 'L0_cond_ln_g': _L0_cond_in['ln_g'], 'L0_cond_ln_b': _L0_cond_in['ln_b'], 'L0_cond_ada_w': _L0_cond_in['ada_w'], 'L0_cond_ada_b': _L0_cond_in['ada_b'], 'L0_cond_in_proj_w': _L0_cond_in['in_proj_w'], 'L0_cond_conv_w': _L0_cond_in['conv_w'], 'L0_cond_conv_b': _L0_cond_in['conv_b'], 'L0_cond_x_proj_w': _L0_cond_in['x_proj_w'], 'L0_cond_dt_proj_w': _L0_cond_in['dt_proj_w'], 'L0_cond_dt_proj_b': _L0_cond_in['dt_proj_b'], 'L0_cond_A_log': _L0_cond_in['A_log'], 'L0_cond_D_param': _L0_cond_in['D_param'], 'L0_cond_out_proj_w': _L0_cond_in['out_proj_w'], 'L1_cond_norm_scale': _L1_cond_in['norm_scale'], 'L1_cond_norm_bias': _L1_cond_in['norm_bias'], 'L1_cond_Wq': _L1_cond_in['Wq'], 'L1_cond_bq': _L1_cond_in['bq'], 'L1_cond_Wk': _L1_cond_in['Wk'], 'L1_cond_bk': _L1_cond_in['bk'], 'L1_cond_Wv': _L1_cond_in['Wv'], 'L1_cond_bv': _L1_cond_in['bv'], 'L1_cond_film_emb_W': _L1_cond_in['film_emb_W'], 'L1_cond_film_emb_b': _L1_cond_in['film_emb_b'], 'L1_cond_film_norm_scale': _L1_cond_in['film_norm_scale'], 'L1_cond_film_norm_bias': _L1_cond_in['film_norm_bias'], 'L1_cond_film_out_W': _L1_cond_in['film_out_W'], 'L1_cond_film_out_b': _L1_cond_in['film_out_b']}

def reference(x, cond_2048, mask_BxS_ik0, L0_cond_ln_g, L0_cond_ln_b, L0_cond_ada_w, L0_cond_ada_b, L0_cond_in_proj_w, L0_cond_conv_w, L0_cond_conv_b, L0_cond_x_proj_w, L0_cond_dt_proj_w, L0_cond_dt_proj_b, L0_cond_A_log, L0_cond_D_param, L0_cond_out_proj_w, L1_cond_norm_scale, L1_cond_norm_bias, L1_cond_Wq, L1_cond_bq, L1_cond_Wk, L1_cond_bk, L1_cond_Wv, L1_cond_bv, L1_cond_film_emb_W, L1_cond_film_emb_b, L1_cond_film_norm_scale, L1_cond_film_norm_bias, L1_cond_film_out_W, L1_cond_film_out_b):
    import jax
    import jax.numpy as jnp

    def _L0_cond_ref(x, c, ln_g, ln_b, ada_w, ada_b, in_proj_w, conv_w, conv_b, x_proj_w, dt_proj_w, dt_proj_b, A_log, D_param, out_proj_w):
        import jax, jax.numpy as jnp
        import numpy as np
        D = 128
        DI = 256
        N = 16
        DT_RANK = 64
        D_CONV = 4
        EPS = 1e-05

        def _layernorm(x, g, b):
            mu = jnp.mean(x, axis=-1, keepdims=True)
            var = jnp.mean((x - mu) ** 2, axis=-1, keepdims=True)
            return (x - mu) * jax.lax.rsqrt(var + EPS) * g + b

        def _mamba(xn, in_proj_w, conv_w, conv_b, x_proj_w, dt_proj_w, dt_proj_b, A_log, D_param, out_proj_w):
            b, sl, _ = xn.shape
            xz = jnp.einsum('bsd,ed->bse', xn, in_proj_w)
            x_in, z = jnp.split(xz, 2, axis=-1)
            xt = jnp.transpose(x_in, (0, 2, 1))
            u = jax.lax.conv_general_dilated(xt, conv_w[:, None, :], (1,), [(D_CONV - 1, 0)], feature_group_count=DI, dimension_numbers=('NCH', 'OIH', 'NCH')) + conv_b[None, :, None]
            u = jax.nn.silu(jnp.transpose(u, (0, 2, 1)))
            x_dbl = jnp.einsum('bsd,ed->bse', u, x_proj_w)
            dt_r, B, C = jnp.split(x_dbl, [DT_RANK, DT_RANK + N], axis=-1)
            dt = jax.nn.softplus(jnp.einsum('bsr,dr->bsd', dt_r, dt_proj_w) + dt_proj_b)
            A = -jnp.exp(A_log)

            def step(h, inp):
                dt_t, B_t, C_t, u_t = inp
                dA = jnp.exp(dt_t[:, :, None] * A)
                h = h * dA + (dt_t * u_t)[:, :, None] * B_t[:, None, :]
                y = jnp.einsum('bdn,bn->bd', h, C_t)
                return (h, y)
            seq = (jnp.transpose(dt, (1, 0, 2)), jnp.transpose(B, (1, 0, 2)), jnp.transpose(C, (1, 0, 2)), jnp.transpose(u, (1, 0, 2)))
            h0 = jnp.zeros((b, DI, N), xn.dtype)
            _, ys = jax.lax.scan(step, h0, seq)
            y = jnp.transpose(ys, (1, 0, 2)) + u * D_param
            y = y * jax.nn.silu(z)
            return jnp.einsum('bsd,ed->bse', y, out_proj_w)
        ada = jnp.einsum('bc,ec->be', jax.nn.silu(c), ada_w) + ada_b
        shift, scale, gate = jnp.split(ada, 3, axis=1)
        xn = _layernorm(x, ln_g, ln_b)
        xn = xn * (1.0 + scale[:, None, :]) + shift[:, None, :]
        x_ssm = _mamba(xn, in_proj_w, conv_w, conv_b, x_proj_w, dt_proj_w, dt_proj_b, A_log, D_param, out_proj_w)
        return x + gate[:, None, :] * x_ssm

    def _L1_cond_ref(x, emb, src_mask, norm_scale, norm_bias, Wq, bq, Wk, bk, Wv, bv, film_emb_W, film_emb_b, film_norm_scale, film_norm_bias, film_out_W, film_out_b):
        import jax, jax.numpy as jnp
        import numpy as np
        H = 16
        LN_EPS = 1e-05

        def _layernorm(x, scale, bias):
            mu = jnp.mean(x, axis=-1, keepdims=True)
            var = jnp.var(x, axis=-1, keepdims=True)
            return (x - mu) * jax.lax.rsqrt(var + LN_EPS) * scale + bias
        B, T, D = x.shape
        dh = D // H
        xn = _layernorm(x, norm_scale, norm_bias)
        q = xn @ Wq + bq
        k = xn @ Wk + bk
        v = xn @ Wv + bv
        mask = (src_mask == 1)[:, :, None]
        k = jnp.where(mask, -jnp.inf, k)
        v = jnp.where(mask, 0.0, v)
        q = q.reshape(B, T, H, dh).transpose(0, 2, 1, 3)
        k = k.reshape(B, T, H, dh).transpose(0, 2, 1, 3)
        v = v.reshape(B, T, H, dh).transpose(0, 2, 1, 3)
        q = jax.nn.softmax(q, axis=-1)
        k = jax.nn.softmax(k, axis=2)
        attn = jnp.einsum('bhse,bhsd->bhed', k, v)
        y = jnp.einsum('bhtd,bhed->bhte', q, attn)
        y = y.transpose(0, 2, 1, 3).reshape(B, T, D)
        emb_out = jax.nn.silu(emb) @ film_emb_W + film_emb_b
        scale, shift = jnp.split(emb_out, 2, axis=-1)
        h = _layernorm(y, film_norm_scale, film_norm_bias) * (1.0 + scale[:, None, :]) + shift[:, None, :]
        h = jax.nn.silu(h) @ film_out_W + film_out_b
        return x + h
    x = _L0_cond_ref(x, cond_2048, L0_cond_ln_g, L0_cond_ln_b, L0_cond_ada_w, L0_cond_ada_b, L0_cond_in_proj_w, L0_cond_conv_w, L0_cond_conv_b, L0_cond_x_proj_w, L0_cond_dt_proj_w, L0_cond_dt_proj_b, L0_cond_A_log, L0_cond_D_param, L0_cond_out_proj_w)
    x = _L1_cond_ref(x, cond_2048, mask_BxS_ik0, L1_cond_norm_scale, L1_cond_norm_bias, L1_cond_Wq, L1_cond_bq, L1_cond_Wk, L1_cond_bk, L1_cond_Wv, L1_cond_bv, L1_cond_film_emb_W, L1_cond_film_emb_b, L1_cond_film_norm_scale, L1_cond_film_norm_bias, L1_cond_film_out_W, L1_cond_film_out_b)
    return x

_drawn_inputs = setup_inputs


def setup_inputs(seed=0):
    import zlib

    import numpy as np

    out = dict(_drawn_inputs(seed))
    spreads = {'L0_cond_ln_g': (1.0, 0.2),
     'L0_cond_ln_b': (0.0, 0.1),
     'L0_cond_ada_b': (0.0, 0.1),
     'L0_cond_conv_b': (0.0, 0.1),
     'L0_cond_D_param': (1.0, 0.2),
     'L1_cond_norm_scale': (1.0, 0.6),
     'L1_cond_norm_bias': (0.0, 0.39),
     'L1_cond_bq': (0.0, 0.76),
     'L1_cond_bk': (0.0, 2.0),
     'L1_cond_bv': (0.0, 0.1),
     'L1_cond_film_emb_b': (0.0, 0.532),
     'L1_cond_film_norm_scale': (1.0, 0.572),
     'L1_cond_film_norm_bias': (0.0, 0.549),
     'L1_cond_film_out_b': (0.0, 0.1)}
    factors = {'L1_cond_Wk': 4.392}
    for name, (base, spread) in spreads.items():
        noise = np.random.default_rng([zlib.crc32(name.encode()), seed]).standard_normal(out[name].shape)
        drawn = base * np.exp(spread * noise) if base else spread * noise
        out[name] = jnp.asarray(drawn.astype(out[name].dtype))
    for name, factor in factors.items():
        out[name] = (out[name] * factor).astype(out[name].dtype)
    return out
```

```python
import concourse.bass as bass
from concourse import mybir
from contextlib import ExitStack

B, S, D = 32, 32, 128
DI, N, R, CONV = 256, 16, 64, 4
HEAD = 8
E = 256
EPS = 1e-5
P = 128
HALVES = DI // P
CHUNKS = 2
CB_ = B // CHUNKS
CT = CB_ * S
TILES = CT // P
TB = P // S
KC = E // P
PARTS = 3
BCR = 2 * N
MASKED = -1e30

PACK_ADA = [("cond", KC * B), ("ada_w", KC * 3 * D), ("ada_b", 3), ("ln_g", 1), ("ln_b", 1)]
PACK_SSM = [("ident", P), ("in_w", 2 * DI), ("conv_w", HALVES * CONV), ("conv_b", HALVES), ("xp_dt", HALVES * R),
            ("xp_bc", HALVES * PARTS * BCR), ("dt_w", DI), ("dt_b", HALVES), ("a_log", HALVES * N),
            ("d_skip", HALVES), ("sel_seed", BCR)]
PACK_ATT = [("out_w", HALVES * D), ("norm_s", 1), ("norm_b", 1), ("wq", D), ("wk", D), ("wv", D),
            ("film_w", KC * 2 * D), ("film_b", 2), ("fnorm_s", 1), ("fnorm_b", 1), ("fo_w", D), ("heads", D)]


def columns(pack):
    at, out = 0, {}
    for name, width in pack:
        out[name] = (at, at + width)
        at += width
    return out, at


def mamba_attention_kernel(nc, x, pack_ada, pack_ssm, pack_att, rows, key_rows, mask_row, mask_tok, film_ob, out):
    fp32, bf16, i32 = mybir.dt.float32, mybir.dt.bfloat16, mybir.dt.int32
    ALU, ACT, AX = mybir.AluOpType, mybir.ActivationFunctionType, mybir.AxisListType

    with ExitStack() as ctx:
        def sb(name, shape, dt=fp32):
            return ctx.enter_context(nc.sbuf_tensor(name, shape, dt))

        def pb(name, shape):
            return ctx.enter_context(nc.psum_tensor(name, shape, fp32))

        def sem(name):
            return ctx.enter_context(nc.semaphore(name))

        x_sb = sb("x_sb", [P, CHUNKS * TILES, D])
        at_ada, n_ada = columns(PACK_ADA)
        at_ssm, n_ssm = columns(PACK_SSM)
        at_att, n_att = columns(PACK_ATT)
        ada_sb = sb("ada_sb", [P, n_ada])
        ssm_sb = sb("ssm_sb", [P, n_ssm])
        att_sb = sb("att_sb", [P, n_att])
        rows_sb = sb("rows_sb", [1, 3 * D])
        key_lhs = sb("key_lhs", [2, D])
        key_rhs = sb("key_rhs", [2, B * S])
        mask_row_i = sb("mask_row_i", [1, B * S], i32)
        mask_tok_i = sb("mask_tok_i", [P, CHUNKS * TILES], i32)
        film_ob_bc = sb("film_ob_bc", [P, D])

        def ada(name):
            return ada_sb[:, at_ada[name][0]:at_ada[name][1]]

        def ssm(name):
            return ssm_sb[:, at_ssm[name][0]:at_ssm[name][1]]

        def att(name):
            return att_sb[:, at_att[name][0]:at_att[name][1]]

        cond_in = ada("cond")
        ada_w = ada("ada_w").rearrange("p (k e) -> p k e", k=KC)
        ident = ssm("ident")
        in_w = ssm("in_w").rearrange("p (m e) -> p m e", e=P)
        conv_w = ssm("conv_w").rearrange("p (h k) -> p h k", h=HALVES)
        conv_b = ssm("conv_b")
        xp_dt = ssm("xp_dt").rearrange("p (h r) -> p h r", h=HALVES)
        xp_bc = ssm("xp_bc").rearrange("p (h r) -> p h r", h=HALVES)
        dt_w = ssm("dt_w")[0:R, :].rearrange("r (h d) -> r h d", h=HALVES)
        dt_b = ssm("dt_b")
        a_log = ssm("a_log")
        d_skip = ssm("d_skip")
        sel_seed = ssm("sel_seed")[0:PARTS * BCR, :]
        out_w = att("out_w").rearrange("p (h e) -> p h e", h=HALVES)
        film_w = att("film_w").rearrange("p (k e) -> p k e", k=KC)
        heads = att("heads")
        bq_row, bv_row, ones_row = (rows_sb[0:1, i * D:(i + 1) * D] for i in range(3))

        cond_s = sb("cond_s", [P, KC, B])
        adas = sb("adas", [P, 3, B])
        ln_tmp = sb("ln_tmp", [P, B])
        ln_mul = sb("ln_mul", [P, B])
        ln_add = sb("ln_add", [P, B])
        films = sb("films", [P, 2, B])
        film_tmp = sb("film_tmp", [P, B])
        film_mul = sb("film_mul", [P, B])
        film_add = sb("film_add", [P, B])
        gate_x = sb("gate_x", [P, B * S])
        gate_tok = sb("gate_tok", [P, CHUNKS * TILES, D])
        a_exp = sb("a_exp", [P, HALVES * N])
        a_neg = sb("a_neg", [P, HALVES * N])
        sel = sb("sel", [PARTS * BCR, BCR, P], bf16)
        diag_d = sb("diag_d", [P, HALVES, P])
        valid = sb("valid", [P, CHUNKS * TILES])
        half_neg = sb("half_neg", [P, TILES])

        def per_chunk(name, shape, dt=fp32):
            return [sb(f"{name}{c}", shape, dt) for c in range(CHUNKS)]

        def shared(name, shape, dt=fp32):
            return [sb(name, shape, dt)] * CHUNKS

        def norm_buffers(name, per_chunk):
            return {"stats": per_chunk(name + "_stats", [P, TILES, 6]), "mv": per_chunk(name + "_mv", [P, TILES, 2]),
                    "var": per_chunk(name + "_var", [P, TILES]), "rstd": per_chunk(name + "_rstd", [P, TILES]),
                    "hat": per_chunk(name + "_hat", [P, TILES, D])}

        ln0, ln1, ln2 = norm_buffers("ln0", per_chunk), norm_buffers("ln1", shared), norm_buffers("ln2", shared)
        xn = per_chunk("xn", [P, CT])
        u = per_chunk("u", [P, HALVES, CT])
        z_s = per_chunk("z_s", [P, HALVES, CT])
        bc_parts = per_chunk("bc_parts", [PARTS * BCR, CT], bf16)
        bc_rest = per_chunk("bc_rest", [PARTS * BCR, CT])
        dt_r = per_chunk("dt_r", [R, CT])
        sp = shared("sp", [P, HALVES, CT])
        dt = per_chunk("dt", [P, HALVES, CT])
        dtu = per_chunk("dtu", [P, HALVES, CT])
        g = shared("g", [P, HALVES, CT])
        x1 = shared("x1", [P, TILES, D])
        x1b = shared("x1b", [P, TILES, D])
        x1n = shared("x1n", [P, CT])
        k_max = shared("k_max", [P, CB_])
        k_exp = shared("k_exp", [P, CT])
        k_sum = shared("k_sum", [P, CB_])
        k_den = shared("k_den", [P, CB_])
        k_inv = shared("k_inv", [P, CB_])
        k_soft = shared("k_soft", [P, CT])
        q_max = shared("q_max", [P, TILES * D // HEAD])
        q_exp = shared("q_exp", [P, TILES * D])
        q_sum = shared("q_sum", [P, TILES * D // HEAD])
        q_inv = shared("q_inv", [P, TILES * D // HEAD])
        v_sb = shared("v_sb", [P, TILES, D])
        q_cm = shared("q_cm", [P, CT])
        k_big = sb("k_big", [P, TILES, TB, D])
        kv = sb("kv", [P, TILES, TB, D])
        y1 = shared("y1", [P, TILES, D])
        fh = shared("fh", [P, CT])
        res = per_chunk("res", [P, TILES, D])

        RD, RB, RH, RC = 3, 3, 3, 3
        decay = sb("decay", [P, RD, HALVES, CT])
        b_bc = sb("b_bc", [P, RB, CT])
        drive = sb("drive", [P, RD, HALVES, CT])
        state = sb("state", [P, RH, HALVES, CT])
        hc = sb("hc", [P, RC, HALVES, CT])

        y_ps = [pb(f"y_ps{h}", [P, CT]) for h in range(HALVES)]
        c_ps = [pb(f"c_ps{i}", [P, CT]) for i in range(2)]
        b_ps = pb("b_ps", [P, CT])
        w0, w1, w2 = (pb(f"w{i}", [P, CT]) for i in range(3))

        x_in = [sem(f"x_in{c}") for c in range(CHUNKS)]
        ada_in, ssm_in, att_in, row_in, mask_in, out_done = (
            sem(n) for n in ("ada_in", "ssm_in", "att_in", "row_in", "mask_in", "out_done"))
        names = """cleared const_gp cond_ready ada_mm ada_biased ln_tmp_ready ln_affine gate_spread gate_mm gate_ready film_mm
            film_biased film_affine a_exp_ready a_ready mask_ready
            stat0 aggr0 var0 rstd0 hat0 hat0_T xg_ready xn_ready x_mm z_mm conv_first conv_tap u_ready z_ready
            bc_mm bc_top bc_rest_ready bc_mid bc_ready dtr_mm dtr_ready dt_mm sp_abs sp_relu sp_exp_ready sp_ready dt_ready
            dtu_ready b_mm b_copied drive_ready decay_ready scan_done c_mm hc_ready y_mm
            g_ready proj_mm gated_ready x1_ready x1b_ready stat1 aggr1 var1 rstd1 hat1 hat1_T x1n_ready
            k_mm k_max_ready k_sub_ready k_exp_ready k_sum_ready k_den_ready k_inv_ready k_soft_ready
            q_mm q_max_ready q_sub_ready q_exp_ready q_sum_ready q_inv_ready v_mm v_ready
            q_T q_cm_ready k_T k_big_ready kv_mm kv_ready y1_mm y1_ready
            stat2 aggr2 var2 rstd2 hat2 hat2_T fm_ready fh_ready fs_ready fo_mm res_ready""".split()
        s = {name: sem(name) for name in names}

        def batches(ap):
            return ap.rearrange("p (b t) -> p b t", t=S)

        def over_steps(ap):
            return ap.unsqueeze(2).broadcast_to([P, CB_, S])

        def over_head(ap):
            return ap.unsqueeze(2).broadcast_to([P, TILES * D // HEAD, HEAD])

        def in_heads(ap):
            return ap.rearrange("p (g e) -> p g e", e=HEAD)

        def mine(c):
            return slice(c * CB_, (c + 1) * CB_)

        def tiled(ap):
            return ap.rearrange("p (t e) -> p t e", e=D)

        block = ctx.enter_context(nc.Block())

        @block.sync
        def _(sync):
            x_v = x.rearrange("(n p) d -> p n d", p=P)
            sync.dma_start(x_sb[:, 0:TILES, :], x_v[:, 0:TILES, :]).then_inc(x_in[0], 16)
            sync.dma_start(ssm_sb[:, :], pack_ssm).then_inc(ssm_in, 16)
            sync.dma_start(x_sb[:, TILES:, :], x_v[:, TILES:, :]).then_inc(x_in[1], 16)
            sync.dma_start(mask_row_i[:, :], mask_row).then_inc(mask_in, 16)
            sync.dma_start(mask_tok_i[:, :], mask_tok).then_inc(mask_in, 16)
            out_v = out.rearrange("(n p) d -> p n d", p=P)
            for c in range(CHUNKS):
                sync.wait_ge(s["res_ready"], c + 1)
                sync.dma_start(out_v[:, c * TILES:(c + 1) * TILES, :], res[c][:, :, :]).then_inc(out_done, 16)
            sync.wait_ge(out_done, 16 * CHUNKS)

        @block.gpsimd
        def _(gp):
            tt, ts = nc.gpsimd.tensor_tensor, nc.gpsimd.tensor_scalar

            def rstd(k, buf, c):
                gp.wait_ge(s[f"var{k}"], c + 1)
                if k == 0 and c == 0:
                    gp.wait_ge(s["cleared"], 4)
                tt(buf["rstd"][c][:, :], buf["var"][c][:, :], half_neg[:, :], ALU.pow).then_inc(s[f"rstd{k}"], 1)

            def drive_step(i):
                c = i // N
                if i % N == 0:
                    gp.wait_ge(s["dtu_ready"], HALVES * (c + 1))
                gp.wait_ge(s["b_copied"], i + 1)
                if i >= RD:
                    gp.wait_ge(s["scan_done"], i - RD + 1)
                tt(drive[:, i % RD, :, :], dtu[c][:, :, :],
                   b_bc[:, i % RB, :].unsqueeze(1).broadcast_to([P, HALVES, CT]), ALU.mult).then_inc(s["drive_ready"], 1)

            nc.gpsimd.memset(half_neg[:, :], -0.5).then_inc(s["cleared"], 1)
            nc.gpsimd.memset(decay[:, :, :, :].rearrange("p r h (b t) -> p (r h b) t", t=S)[:, :, 0:1], 0.0)\
                .then_inc(s["cleared"], 1)
            nc.gpsimd.memset(key_rhs[:, :], 1.0).then_inc(s["cleared"], 1)
            nc.gpsimd.memset(k_big[:, :, :, :], 0.0).then_inc(s["cleared"], 1)
            rstd(0, ln0, 0)
            gp.wait_ge(ssm_in, 16)
            ts(sel[:, :, :], sel_seed.unsqueeze(2).broadcast_to([PARTS * BCR, BCR, P]), 1.0, 0.0, ALU.mult, ALU.add)\
                .then_inc(s["const_gp"], 1)
            for h in range(HALVES):
                ts(diag_d[:, h, :], ident, d_skip[:, h:h + 1], 0.0, ALU.mult, ALU.add).then_inc(s["const_gp"], 1)

            def late_sums(c):
                gp.wait_ge(s["x1_ready"], c + 1)
                gp.wait_ge(row_in, 48)
                tt(x1b[c][:, :, :], x1[c][:, :, :], film_ob_bc[:, :].unsqueeze(1).broadcast_to([P, TILES, D]),
                   ALU.add).then_inc(s["x1b_ready"], 1)

            def soft_keys(c):
                gp.wait_ge(s["k_inv_ready"], c + 1)
                tt(batches(k_soft[c][:, :]), batches(k_exp[c][:, :]), over_steps(k_inv[c][:, :]), ALU.mult)\
                    .then_inc(s["k_soft_ready"], 1)

            gp.dma_start(rows_sb[:, :], rows).then_inc(row_in, 16)
            gp.dma_start(key_lhs[:, :], key_rows).then_inc(row_in, 16)
            gp.dma_start(film_ob_bc[:, :], film_ob.partition_broadcast(P)).then_inc(row_in, 16)
            drive_step(0)
            for i in range(CHUNKS * N):
                c, n = i // N, i % N
                if i + 1 < CHUNKS * N:
                    drive_step(i + 1)
                if c == 0 and n == 0:
                    rstd(0, ln0, 1)
                if c == 1 and n == 2:
                    rstd(1, ln1, 0)
                if c == 1 and n == 6:
                    soft_keys(0)
                if c == 1 and n == 8:
                    late_sums(0)
                if c == 1 and n == 12:
                    rstd(2, ln2, 0)
            rstd(1, ln1, 1)
            soft_keys(1)
            late_sums(1)
            rstd(2, ln2, 1)

        @block.scalar
        def _(act):
            A = nc.scalar.activation
            act.dma_start(ada_sb[:, :], pack_ada).then_inc(ada_in, 16)
            act.dma_start(att_sb[:, :], pack_att).then_inc(att_in, 16)

            act.wait_ge(ada_in, 16)
            A(cond_s[:, :, :].rearrange("p k b -> p (k b)"), cond_in, ACT.Silu).then_inc(s["cond_ready"], 1)

            def conv_start(c):
                for h, bank in enumerate((w1, w2)):
                    act.wait_ge(s["x_mm"], HALVES * c + h + 1)
                    A(u[c][:, h, :], bank[:, :], ACT.Identity, bias=conv_b[:, h:h + 1],
                      scale=conv_w[:, h, CONV - 1:CONV]).then_inc(s["conv_first"], 1)

            def silu_u(c):
                for h in range(HALVES):
                    act.wait_ge(s["conv_tap"], HALVES * (CONV - 1) * c + HALVES * (CONV - 2) + h + 1)
                    A(u[c][:, h, :], u[c][:, h, :], ACT.Silu).then_inc(s["u_ready"], 1)

            def silu_z(c, banks):
                for h, bank in enumerate(banks):
                    act.wait_ge(s["z_mm"], HALVES * c + h + 1)
                    A(z_s[c][:, h, :], bank[:, :], ACT.Silu).then_inc(s["z_ready"], 1)

            def copy_dt_rows(c):
                act.wait_ge(s["dtr_mm"], c + 1)
                A(dt_r[c][:, :], w0[0:R, :], ACT.Copy).then_inc(s["dtr_ready"], 1)

            def top_bc(c):
                act.wait_ge(s["bc_mm"], c + 1)
                A(bc_parts[c][:, :], w0[0:PARTS * BCR, :], ACT.Copy).then_inc(s["bc_top"], 1)

            def softplus(c):
                for h, bank in enumerate((w1, w2)):
                    act.wait_ge(s["dt_mm"], HALVES * c + h + 1)
                    A(sp[c][:, h, :], bank[:, :], ACT.Abs, bias=dt_b[:, h:h + 1]).then_inc(s["sp_abs"], 1)
                    if c:
                        A(dt[c][:, h, :], bank[:, :], ACT.Relu, bias=dt_b[:, h:h + 1]).then_inc(s["sp_relu"], 1)
                act.wait_ge(s["sp_abs"], HALVES * (c + 1))
                for h in range(HALVES):
                    A(sp[c][:, h, :], sp[c][:, h, :], ACT.Exp, scale=-1.0).then_inc(s["sp_exp_ready"], 1)
                for h in range(HALVES):
                    act.wait_ge(s["sp_exp_ready"], HALVES * c + h + 1)
                    A(sp[c][:, h, :], sp[c][:, h, :], ACT.Ln, bias=1.0).then_inc(s["sp_ready"], 1)

            def decays(i):
                c, n = i // N, i % N
                if n == 0:
                    act.wait_ge(s["dt_ready"], HALVES * (c + 1))
                    act.wait_ge(s["a_ready"], 1)
                    act.wait_ge(s["cleared"], 2)
                if i >= RD:
                    act.wait_ge(s["scan_done"], i - RD + 1)
                for h in range(HALVES):
                    A(batches(decay[:, i % RD, h, :])[:, :, 1:S], batches(dt[c][:, h, :])[:, :, 1:S], ACT.Exp,
                      scale=a_neg[:, h * N + n:h * N + n + 1]).then_inc(s["decay_ready"], 1)

            def copy_b(i):
                act.wait_ge(s["b_mm"], i + 1)
                if i >= RB:
                    act.wait_ge(s["drive_ready"], i - RB + 1)
                A(b_bc[:, i % RB, :], b_ps[:, :], ACT.Copy).then_inc(s["b_copied"], 1)

            def x1_affine(c):
                act.wait_ge(s["hat1_T"], c + 1)
                if c == 0:
                    act.wait_ge(att_in, 16)
                A(x1n[c][:, :], w1[:, :], ACT.Identity, bias=att("norm_b"), scale=att("norm_s"))\
                    .then_inc(s["x1n_ready"], 1)

            def values(c):
                act.wait_ge(s["v_mm"], c + 1)
                for t in range(TILES):
                    A(v_sb[c][:, t, :], tiled(w1[:, :])[:, t, :], ACT.Copy, scale=valid[:, c * TILES + t:c * TILES + t + 1])\
                        .then_inc(s["v_ready"], 1)

            def soft_exps(c):
                act.wait_ge(s["k_sub_ready"], c + 1)
                A(k_exp[c][:, :], k_exp[c][:, :], ACT.Exp).then_inc(s["k_exp_ready"], 1)
                act.wait_ge(s["q_sub_ready"], c + 1)
                A(q_exp[c][:, :], q_exp[c][:, :], ACT.Exp).then_inc(s["q_exp_ready"], 1)

            def turned(c):
                act.wait_ge(s["q_T"], c + 1)
                A(q_cm[c][:, :], w0[:, :], ACT.Copy).then_inc(s["q_cm_ready"], 1)
                act.wait_ge(s["k_T"], c + 1)
                act.wait_ge(s["cleared"], 4)
                if c:
                    act.wait_ge(s["kv_mm"], TILES * c)
                for j in range(TB):
                    A(k_big[j * S:(j + 1) * S, :, j, :], tiled(w2[j * S:(j + 1) * S, :]), ACT.Copy)\
                        .then_inc(s["k_big_ready"], 1)

            def film_silu(c):
                act.wait_ge(s["fh_ready"], c + 1)
                A(fh[c][:, :], fh[c][:, :], ACT.Silu).then_inc(s["fs_ready"], 1)

            conv_start(0)
            silu_z(0, y_ps)
            silu_u(0)
            copy_dt_rows(0)
            nc.scalar.preload_act_table_set("natural_log_exp_and_others")
            A(a_exp[:, :], a_log, ACT.Exp).then_inc(s["a_exp_ready"], 1)
            softplus(0)
            top_bc(0)
            decays(0)
            copy_b(0)
            copy_b(1)
            for i in range(CHUNKS * N):
                c, n = i // N, i % N
                if i + 2 < CHUNKS * N:
                    copy_b(i + 2)
                if i + 1 < CHUNKS * N:
                    decays(i + 1)
                if c == 0 and n == 3:
                    conv_start(1)
                if c == 0 and n == 6:
                    silu_z(1, (w0, w1))
                    silu_u(1)
                    nc.scalar.preload_act_table_set("natural_log_exp_and_others")
                if c == 0 and n == 7:
                    copy_dt_rows(1)
                if c == 0 and n == 8:
                    softplus(1)
                if c == 0 and n == 9:
                    top_bc(1)
                if c == 1 and n == 3:
                    x1_affine(0)
                if c == 1 and n == 5:
                    values(0)
                    soft_exps(0)
                if c == 1 and n == 7:
                    turned(0)
                if c == 1 and n == 14:
                    film_silu(0)
                    nc.scalar.preload_act_table_set("natural_log_exp_and_others")
            x1_affine(1)
            values(1)
            soft_exps(1)
            turned(1)
            film_silu(1)

        @block.vector
        def _(dve):
            V = nc.vector

            def norm_stats(k, buf, c, src):
                for t in range(TILES):
                    V.bn_stats(buf["stats"][c][:, t, :], src(t)).then_inc(s[f"stat{k}"], 1)
                dve.wait_ge(s[f"stat{k}"], TILES * (c + 1))
                for t in range(TILES):
                    V.bn_aggr(buf["mv"][c][:, t, :], buf["stats"][c][:, t, :]).then_inc(s[f"aggr{k}"], 1)
                dve.wait_ge(s[f"aggr{k}"], TILES * (c + 1))
                V.tensor_scalar(buf["var"][c][:, :], buf["mv"][c][:, :, 1:2].rearrange("p t o -> p (t o)"), EPS, None,
                                ALU.add).then_inc(s[f"var{k}"], 1)

            def normalise(k, buf, c, src):
                dve.wait_ge(s[f"rstd{k}"], c + 1)
                for t in range(TILES):
                    V.tensor_scalar(buf["hat"][c][:, t, :], src(t), buf["mv"][c][:, t, 0:1], buf["rstd"][c][:, t:t + 1],
                                    ALU.subtract, ALU.mult).then_inc(s[f"hat{k}"], 1)

            def x_tile(c):
                return lambda t: x_sb[:, c * TILES + t, :]

            def adaptive(c):
                dve.wait_ge(s["hat0_T"], c + 1)
                V.tensor_tensor(batches(xn[c][:, :]), batches(w0[:, :]), over_steps(ln_mul[:, mine(c)]), ALU.mult)\
                    .then_inc(s["xg_ready"], 1)
                dve.wait_ge(s["xg_ready"], c + 1)
                V.tensor_tensor(batches(xn[c][:, :]), batches(xn[c][:, :]), over_steps(ln_add[:, mine(c)]), ALU.add)\
                    .then_inc(s["xn_ready"], 1)

            def conv_taps(c):
                for back in range(1, CONV):
                    for h, bank in enumerate((w1, w2)):
                        if back == 1:
                            dve.wait_ge(s["conv_first"], HALVES * c + h + 1)
                        else:
                            dve.wait_ge(s["conv_tap"], HALVES * ((CONV - 1) * c + back - 2) + h + 1)
                        V.scalar_tensor_tensor(
                            out=batches(u[c][:, h, :])[:, :, back:S], in0=batches(bank[:, :])[:, :, 0:S - back],
                            scalar=conv_w[:, h, CONV - 1 - back:CONV - back],
                            in1=batches(u[c][:, h, :])[:, :, back:S], op0=ALU.mult, op1=ALU.add)\
                            .then_inc(s["conv_tap"], 1)

            def split_bc(c):
                dve.wait_ge(s["bc_top"], c + 1)
                V.tensor_tensor(bc_rest[c][:, :], w0[0:PARTS * BCR, :], bc_parts[c][:, :], ALU.subtract)\
                    .then_inc(s["bc_rest_ready"], 1)
                dve.wait_ge(s["bc_rest_ready"], c + 1)
                for part in range(1, PARTS):
                    r = slice(part * BCR, (part + 1) * BCR)
                    V.tensor_copy(bc_parts[c][r, :], bc_rest[c][r, :]).then_inc(s["bc_mid"], 1)
                dve.wait_ge(s["bc_mid"], 2 * (c + 1))
                V.tensor_tensor(bc_parts[c][r, :], bc_rest[c][r, :], bc_parts[c][r, :], ALU.subtract)\
                    .then_inc(s["bc_ready"], 1)

            def relu_dt(c):
                for h, bank in enumerate((w1, w2)):
                    dve.wait_ge(s["sp_abs"], HALVES * c + h + 1)
                    V.tensor_scalar(dt[c][:, h, :], bank[:, :], dt_b[:, h:h + 1], 0.0, ALU.add, ALU.max)\
                        .then_inc(s["sp_relu"], 1)

            def steps(c):
                dve.wait_ge(s["sp_relu"], HALVES * (c + 1))
                for h in range(HALVES):
                    dve.wait_ge(s["sp_ready"], HALVES * c + h + 1)
                    V.tensor_tensor(dt[c][:, h, :], sp[c][:, h, :], dt[c][:, h, :], ALU.add).then_inc(s["dt_ready"], 1)
                dve.wait_ge(s["u_ready"], HALVES * (c + 1))
                for h in range(HALVES):
                    dve.wait_ge(s["dt_ready"], HALVES * c + h + 1)
                    V.tensor_tensor(dtu[c][:, h, :], dt[c][:, h, :], u[c][:, h, :], ALU.mult).then_inc(s["dtu_ready"], 1)

            def scan(i):
                dve.wait_ge(s["decay_ready"], HALVES * (i + 1))
                dve.wait_ge(s["drive_ready"], i + 1)
                if i >= RH:
                    dve.wait_ge(s["hc_ready"], i - RH + 1)
                V.tensor_tensor_scan(state[:, i % RH, :, :].rearrange("p h t -> p (h t)"),
                                     decay[:, i % RD, :, :].rearrange("p h t -> p (h t)"),
                                     drive[:, i % RD, :, :].rearrange("p h t -> p (h t)"),
                                     0.0, ALU.mult, ALU.add).then_inc(s["scan_done"], 1)

            def weigh(i):
                dve.wait_ge(s["scan_done"], i + 1)
                dve.wait_ge(s["c_mm"], i + 1)
                if i >= RC:
                    dve.wait_ge(s["y_mm"], i - RC + 1)
                V.tensor_tensor(hc[:, i % RC, :, :], state[:, i % RH, :, :],
                                c_ps[i % 2][:, :].unsqueeze(1).broadcast_to([P, HALVES, CT]), ALU.mult)\
                    .then_inc(s["hc_ready"], 1)

            def gate_z(c):
                dve.wait_ge(s["y_mm"], N * (c + 1))
                dve.wait_ge(s["z_ready"], HALVES * (c + 1))
                for h in range(HALVES):
                    V.tensor_tensor(g[c][:, h, :], y_ps[h][:, :], z_s[c][:, h, :], ALU.mult).then_inc(s["g_ready"], 1)

            def residual(c):
                dve.wait_ge(s["proj_mm"], c + 1)
                dve.wait_ge(s["gate_ready"], 2)
                V.tensor_tensor(x1[c][:, :, :], tiled(w0[:, :]), gate_tok[:, c * TILES:(c + 1) * TILES, :], ALU.mult)\
                    .then_inc(s["gated_ready"], 1)
                dve.wait_ge(s["gated_ready"], c + 1)
                V.tensor_tensor(x1[c][:, :, :], x1[c][:, :, :], x_sb[:, c * TILES:(c + 1) * TILES, :], ALU.add)\
                    .then_inc(s["x1_ready"], 1)
                dve.wait_ge(s["x1_ready"], c + 1)
                norm_stats(1, ln1, c, lambda t: x1[c][:, t, :])

            def keys(c):
                dve.wait_ge(s["k_mm"], c + 1)
                V.tensor_reduce(k_max[c][:, :], batches(w2[:, :]), op=ALU.max, axis=AX.X).then_inc(s["k_max_ready"], 1)
                dve.wait_ge(s["k_max_ready"], c + 1)
                V.tensor_tensor(batches(k_exp[c][:, :]), batches(w2[:, :]), over_steps(k_max[c][:, :]), ALU.subtract)\
                    .then_inc(s["k_sub_ready"], 1)

            def queries(c):
                dve.wait_ge(s["q_mm"], c + 1)
                V.tensor_reduce(q_max[c][:, :], in_heads(w0[:, :]), op=ALU.max, axis=AX.X).then_inc(s["q_max_ready"], 1)
                dve.wait_ge(s["q_max_ready"], c + 1)
                V.tensor_tensor(in_heads(q_exp[c][:, :]), in_heads(w0[:, :]), over_head(q_max[c][:, :]), ALU.subtract)\
                    .then_inc(s["q_sub_ready"], 1)

            def key_sums(c):
                dve.wait_ge(s["k_exp_ready"], c + 1)
                V.tensor_reduce(k_sum[c][:, :], batches(k_exp[c][:, :]), op=ALU.add, axis=AX.X).then_inc(s["k_sum_ready"], 1)
                dve.wait_ge(s["k_sum_ready"], c + 1)
                V.scalar_tensor_tensor(out=k_den[c][:, :], in0=k_max[c][:, :], scalar=MASKED / 2, in1=k_sum[c][:, :],
                                       op0=ALU.is_ge, op1=ALU.mult).then_inc(s["k_den_ready"], 1)
                dve.wait_ge(s["k_den_ready"], c + 1)
                V.reciprocal(k_inv[c][:, :], k_den[c][:, :]).then_inc(s["k_inv_ready"], 1)

            def query_sums(c):
                dve.wait_ge(s["q_exp_ready"], c + 1)
                V.tensor_reduce(q_sum[c][:, :], in_heads(q_exp[c][:, :]), op=ALU.add, axis=AX.X)\
                    .then_inc(s["q_sum_ready"], 1)
                dve.wait_ge(s["q_sum_ready"], c + 1)
                V.reciprocal(q_inv[c][:, :], q_sum[c][:, :]).then_inc(s["q_inv_ready"], 1)

            def head_blocks(c, tiles):
                if c:
                    dve.wait_ge(s["y1_mm"], c)
                for t in tiles:
                    bank = (w1, w2, w0, w1)[t]
                    dve.wait_ge(s["kv_mm"], TILES * c + t + 1)
                    V.tensor_tensor(kv[:, t, :, :], tiled(bank[:, :]), heads.unsqueeze(1).broadcast_to([P, TB, D]),
                                    ALU.mult).then_inc(s["kv_ready"], 1)

            def attended(c):
                dve.wait_ge(s["y1_mm"], c + 1)
                dve.wait_ge(s["q_inv_ready"], c + 1)
                V.tensor_tensor(in_heads(y1[c][:, :, :].rearrange("p t e -> p (t e)")), in_heads(w2[:, :]),
                                over_head(q_inv[c][:, :]), ALU.mult).then_inc(s["y1_ready"], 1)
                dve.wait_ge(s["y1_ready"], c + 1)
                norm_stats(2, ln2, c, lambda t: y1[c][:, t, :])

            def film(c):
                dve.wait_ge(s["hat2_T"], c + 1)
                V.tensor_tensor(batches(fh[c][:, :]), batches(w0[:, :]), over_steps(film_mul[:, mine(c)]), ALU.mult)\
                    .then_inc(s["fm_ready"], 1)
                dve.wait_ge(s["fm_ready"], c + 1)
                V.tensor_tensor(batches(fh[c][:, :]), batches(fh[c][:, :]), over_steps(film_add[:, mine(c)]), ALU.add)\
                    .then_inc(s["fh_ready"], 1)

            def finish(c):
                dve.wait_ge(s["fo_mm"], c + 1)
                dve.wait_ge(s["x1b_ready"], c + 1)
                V.tensor_tensor(res[c][:, :, :], tiled(w1[:, :]), x1b[c][:, :, :], ALU.add).then_inc(s["res_ready"], 1)

            dve.wait_ge(x_in[0], 16)
            norm_stats(0, ln0, 0, x_tile(0))
            normalise(0, ln0, 0, x_tile(0))
            dve.wait_ge(s["ada_mm"], 1)
            V.tensor_tensor(adas[:, :, :], w1[:, 0:3 * B].rearrange("p (m b) -> p m b", b=B),
                            ada("ada_b").unsqueeze(2).broadcast_to([P, 3, B]), ALU.add).then_inc(s["ada_biased"], 1)
            dve.wait_ge(s["ada_biased"], 1)
            V.tensor_scalar(ln_tmp[:, :], adas[:, 1, :], 1.0, ada("ln_b"), ALU.add, ALU.mult).then_inc(s["ln_tmp_ready"], 1)
            V.tensor_scalar(ln_mul[:, :], adas[:, 1, :], 1.0, ada("ln_g"), ALU.add, ALU.mult).then_inc(s["ln_affine"], 1)
            dve.wait_ge(s["ln_tmp_ready"], 1)
            V.tensor_tensor(ln_add[:, :], ln_tmp[:, :], adas[:, 0, :], ALU.add).then_inc(s["ln_affine"], 1)
            dve.wait_ge(s["ln_affine"], 2)
            adaptive(0)
            conv_taps(0)
            dve.wait_ge(s["a_exp_ready"], 1)
            V.tensor_scalar(a_neg[:, :], a_exp[:, :], -1.0, None, ALU.mult).then_inc(s["a_ready"], 1)
            relu_dt(0)
            steps(0)
            split_bc(0)

            def second_constants():
                V.tensor_copy(gate_x[:, :].rearrange("p (b t) -> p b t", t=S),
                              adas[:, 2, :].unsqueeze(2).broadcast_to([P, B, S])).then_inc(s["gate_spread"], 1)
                dve.wait_ge(s["film_mm"], 1)
                V.tensor_tensor(films[:, :, :], w0[:, 0:2 * B].rearrange("p (m b) -> p m b", b=B),
                                att("film_b").unsqueeze(2).broadcast_to([P, 2, B]), ALU.add).then_inc(s["film_biased"], 1)
                dve.wait_ge(s["film_biased"], 1)
                V.tensor_scalar(film_mul[:, :], films[:, 0, :], 1.0, att("fnorm_s"), ALU.add, ALU.mult)\
                    .then_inc(s["film_affine"], 1)
                V.tensor_scalar(film_tmp[:, :], films[:, 0, :], 1.0, att("fnorm_b"), ALU.add, ALU.mult)\
                    .then_inc(s["film_affine"], 1)
                dve.wait_ge(s["film_affine"], 2)
                V.tensor_tensor(film_add[:, :], film_tmp[:, :], films[:, 1, :], ALU.add).then_inc(s["film_affine"], 1)
                dve.wait_ge(mask_in, 32)
                dve.wait_ge(s["cleared"], 3)
                V.tensor_scalar(key_rhs[0:1, :], mask_row_i[:, :], 1.0, MASKED, ALU.is_equal, ALU.mult)\
                    .then_inc(s["mask_ready"], 1)
                V.tensor_scalar(valid[:, :], mask_tok_i[:, :], 1.0, None, ALU.not_equal).then_inc(s["mask_ready"], 1)

            def gates(c, bank):
                dve.wait_ge(s["gate_mm"], c + 1)
                V.tensor_copy(gate_tok[:, c * TILES:(c + 1) * TILES, :], tiled(bank[:, :])).then_inc(s["gate_ready"], 1)

            for i in range(CHUNKS * N):
                c, n = i // N, i % N
                scan(i)
                if n > 0:
                    weigh(i - 1)
                if c == 0 and n == 0:
                    dve.wait_ge(x_in[1], 16)
                    norm_stats(0, ln0, 1, x_tile(1))
                if c == 0 and n == 1:
                    normalise(0, ln0, 1, x_tile(1))
                if c == 0 and n == 2:
                    adaptive(1)
                if c == 0 and n == 4:
                    conv_taps(1)
                if c == 0 and n == 10:
                    split_bc(1)
                    steps(1)
                if c == 0 and n == 12:
                    second_constants()
                if c == 0 and n == 13:
                    gates(0, w1)
                    gates(1, w2)
                if c == 1 and n == 0:
                    weigh(i - 1)
                    gate_z(0)
                if c == 1 and n == 2:
                    residual(0)
                if c == 1 and n == 3:
                    normalise(1, ln1, 0, lambda t: x1[0][:, t, :])
                if c == 1 and n == 5:
                    keys(0)
                    queries(0)
                if c == 1 and n == 6:
                    key_sums(0)
                    query_sums(0)
                if c == 1 and n == 9:
                    head_blocks(0, (0, 1, 2))
                if c == 1 and n == 10:
                    head_blocks(0, (3,))
                if c == 1 and n == 12:
                    attended(0)
                if c == 1 and n == 13:
                    normalise(2, ln2, 0, lambda t: y1[0][:, t, :])
                if c == 1 and n == 14:
                    film(0)
            weigh(CHUNKS * N - 1)
            finish(0)
            gate_z(1)
            residual(1)
            normalise(1, ln1, 1, lambda t: x1[1][:, t, :])
            keys(1)
            queries(1)
            key_sums(1)
            query_sums(1)
            head_blocks(1, range(TILES))
            attended(1)
            normalise(2, ln2, 1, lambda t: y1[1][:, t, :])
            film(1)
            finish(1)

        @block.tensor
        def _(pe):
            mm = nc.tensor.matmul

            def turn(bank, src, done):
                for t in range(TILES):
                    last = nc.tensor.transpose(bank[:, t * P:(t + 1) * P], src(t), ident)
                last.then_inc(done, 1)

            def in_proj(c):
                pe.wait_ge(s["hat0"], TILES * (c + 1))
                if c:
                    pe.wait_ge(s["bc_rest_ready"], c)
                turn(w0, lambda t: ln0["hat"][c][:, t, :], s["hat0_T"])

            def in_proj_x(c):
                pe.wait_ge(s["xn_ready"], c + 1)
                if c:
                    pe.wait_ge(s["sp_relu"], HALVES * c)
                for h, bank in enumerate((w1, w2)):
                    mm(bank[:, :], in_w[:, h, :], xn[c][:, :], start=True, stop=True).then_inc(s["x_mm"], 1)

            def in_proj_z(c, h, bank):
                if c and h:
                    pe.wait_ge(s["conv_tap"], HALVES * (CONV - 1) * (c + 1))
                mm(bank[:, :], in_w[:, HALVES + h, :], xn[c][:, :], start=True, stop=True).then_inc(s["z_mm"], 1)

            def project_dt(c):
                pe.wait_ge(s["u_ready"], HALVES * (c + 1))
                if c:
                    pe.wait_ge(s["z_ready"], HALVES * c + 1)
                for h in range(HALVES):
                    last = mm(w0[0:R, :], xp_dt[:, h, :], u[c][:, h, :], start=(h == 0), stop=(h == HALVES - 1))
                last.then_inc(s["dtr_mm"], 1)

            def dt_proj(c):
                pe.wait_ge(s["dtr_ready"], c + 1)
                if c:
                    pe.wait_ge(s["z_ready"], HALVES * (c + 1))
                for h, bank in enumerate((w1, w2)):
                    mm(bank[:, :], dt_w[:, h, :], dt_r[c][:, :], start=True, stop=True).then_inc(s["dt_mm"], 1)

            def project_bc(c):
                for h in range(HALVES):
                    last = mm(w0[0:PARTS * BCR, :], xp_bc[:, h, :], u[c][:, h, :], start=(h == 0), stop=(h == HALVES - 1))
                last.then_inc(s["bc_mm"], 1)

            def spread_b(i):
                c, n = i // N, i % N
                if n == 0:
                    pe.wait_ge(s["bc_ready"], c + 1)
                if i == 0:
                    pe.wait_ge(s["const_gp"], 1)
                if i >= 1:
                    pe.wait_ge(s["b_copied"], i)
                mm(b_ps[:, :], sel[:, n, :], bc_parts[c][:, :], start=True, stop=True).then_inc(s["b_mm"], 1)

            def spread_c(i):
                c, n = i // N, i % N
                if i >= 2:
                    pe.wait_ge(s["hc_ready"], i - 1)
                mm(c_ps[i % 2][:, :], sel[:, N + n, :], bc_parts[c][:, :], start=True, stop=True).then_inc(s["c_mm"], 1)

            def skip_term(c):
                pe.wait_ge(s["const_gp"], 1 + HALVES)
                if c:
                    pe.wait_ge(s["g_ready"], HALVES * c)
                else:
                    pe.wait_ge(s["z_ready"], HALVES)
                for h in range(HALVES):
                    mm(y_ps[h][:, :], diag_d[:, h, :], u[c][:, h, :], start=True, stop=False)

            def sum_states(i):
                n = i % N
                pe.wait_ge(s["hc_ready"], i + 1)
                for h in range(HALVES):
                    last = mm(y_ps[h][:, :], ident, hc[:, i % RC, h, :], start=False, stop=(n == N - 1))
                last.then_inc(s["y_mm"], 1)

            def out_proj(c):
                pe.wait_ge(s["g_ready"], HALVES * (c + 1))
                if c == 0:
                    pe.wait_ge(s["film_biased"], 1)
                    pe.wait_ge(att_in, 16)
                else:
                    pe.wait_ge(s["fm_ready"], c)
                for t in range(TILES):
                    for h in range(HALVES):
                        last = mm(w0[:, t * D:(t + 1) * D], g[c][:, h, t * P:(t + 1) * P], out_w[:, h, :],
                                  start=(h == 0), stop=(h == HALVES - 1))
                last.then_inc(s["proj_mm"], 1)

            def turn_x1(c):
                pe.wait_ge(s["hat1"], TILES * (c + 1))
                if c == 0:
                    pe.wait_ge(s["gate_ready"], 1)
                else:
                    pe.wait_ge(s["res_ready"], c)
                turn(w1, lambda t: ln1["hat"][c][:, t, :], s["hat1_T"])

            def qkv(c):
                pe.wait_ge(s["x1n_ready"], c + 1)
                pe.wait_ge(row_in, 48)
                pe.wait_ge(s["mask_ready"], 2)
                if c == 0:
                    pe.wait_ge(s["gate_ready"], 2)
                else:
                    pe.wait_ge(s["y1_ready"], c)
                mm(w2[:, :], key_lhs[:, :], key_rhs[:, c * CT:(c + 1) * CT], start=True, stop=False)
                mm(w2[:, :], att("wk"), x1n[c][:, :], start=False, stop=True).then_inc(s["k_mm"], 1)
                pe.wait_ge(s["gated_ready"], c + 1)
                for bank, bias, weight, done in ((w0, bq_row, "wq", "q_mm"), (w1, bv_row, "wv", "v_mm")):
                    for t in range(TILES):
                        o = bank[:, t * D:(t + 1) * D]
                        mm(o, ones_row, bias, start=True, stop=False)
                        last = mm(o, x1n[c][:, t * P:(t + 1) * P], att(weight), start=False, stop=True)
                    last.then_inc(s[done], 1)

            def turn_qk(c):
                pe.wait_ge(s["q_exp_ready"], c + 1)
                turn(w0, lambda t: q_exp[c][:, t * P:(t + 1) * P], s["q_T"])
                pe.wait_ge(s["k_soft_ready"], c + 1)
                turn(w2, lambda t: k_soft[c][:, t * P:(t + 1) * P], s["k_T"])

            def key_values(c, tiles):
                pe.wait_ge(s["v_ready"], TILES * (c + 1))
                pe.wait_ge(s["k_big_ready"], TB * (c + 1))
                pe.wait_ge(s["q_cm_ready"], c + 1)
                for t in tiles:
                    bank = (w1, w2, w0, w1)[t]
                    if t == 3:
                        pe.wait_ge(s["kv_ready"], TILES * c + 1)
                    mm(bank[:, :], v_sb[c][:, t, :], k_big[:, t, :, :].rearrange("p j e -> p (j e)"),
                       start=True, stop=True).then_inc(s["kv_mm"], 1)

            def attend(c):
                for t in range(TILES):
                    pe.wait_ge(s["kv_ready"], TILES * c + max(t + 1, 2))
                    for j in range(TB):
                        last = mm(w2[j * S:(j + 1) * S, t * D:(t + 1) * D],
                                  q_cm[c][:, (t * TB + j) * S:(t * TB + j + 1) * S], kv[:, t, j, :],
                                  start=True, stop=True, tile_position=(0, j * S))
                last.then_inc(s["y1_mm"], 1)

            def turn_y(c):
                pe.wait_ge(s["hat2"], TILES * (c + 1))
                turn(w0, lambda t: ln2["hat"][c][:, t, :], s["hat2_T"])

            def film_out(c):
                pe.wait_ge(s["fs_ready"], c + 1)
                for t in range(TILES):
                    last = mm(w1[:, t * D:(t + 1) * D], fh[c][:, t * P:(t + 1) * P], att("fo_w"), start=True, stop=True)
                last.then_inc(s["fo_mm"], 1)

            def film_factors():
                pe.wait_ge(att_in, 16)
                pe.wait_ge(s["bc_rest_ready"], CHUNKS)
                for m in range(2):
                    for k in range(KC):
                        last = mm(w0[:, m * B:(m + 1) * B], film_w[:, k, m * D:(m + 1) * D], cond_s[:, k, :],
                                  start=(k == 0), stop=(k == KC - 1))
                last.then_inc(s["film_mm"], 1)

            def turn_gate():
                pe.wait_ge(s["gate_spread"], 1)
                pe.wait_ge(s["sp_relu"], HALVES * CHUNKS)
                for c, bank in enumerate((w1, w2)):
                    turn(bank, lambda t: gate_x[:, c * CT + t * P:c * CT + (t + 1) * P], s["gate_mm"])

            pe.wait_ge(ada_in, 16)
            pe.wait_ge(s["cond_ready"], 1)
            for m in range(3):
                for k in range(KC):
                    last = mm(w1[:, m * B:(m + 1) * B], ada_w[:, k, m * D:(m + 1) * D], cond_s[:, k, :],
                              start=(k == 0), stop=(k == KC - 1))
            last.then_inc(s["ada_mm"], 1)
            pe.wait_ge(ssm_in, 16)
            in_proj(0)
            pe.wait_ge(s["ada_biased"], 1)
            in_proj_x(0)
            in_proj_z(0, 0, y_ps[0])
            in_proj_z(0, 1, y_ps[1])
            project_dt(0)
            dt_proj(0)
            project_bc(0)
            for i in range(3):
                spread_b(i)
            spread_c(0)
            for i in range(CHUNKS * N):
                c, n = i // N, i % N
                if i + 1 < CHUNKS * N:
                    spread_c(i + 1)
                if n == 0:
                    if c:
                        sum_states(i - 1)
                    skip_term(c)
                else:
                    sum_states(i - 1)
                if c == 0 and n == 2:
                    in_proj(1)
                if c == 0 and n == 3:
                    in_proj_x(1)
                    in_proj_z(1, 0, w0)
                if c == 0 and n == 5:
                    in_proj_z(1, 1, w1)
                if c == 0 and n == 7:
                    project_dt(1)
                if c == 0 and n == 8:
                    dt_proj(1)
                if c == 0 and n == 9:
                    project_bc(1)
                if c == 0 and n == 12:
                    film_factors()
                    turn_gate()
                if c == 1 and n == 1:
                    out_proj(0)
                if c == 1 and n == 3:
                    turn_x1(0)
                if c == 1 and n == 4:
                    qkv(0)
                if c == 1 and n == 7:
                    turn_qk(0)
                if c == 1 and n == 8:
                    key_values(0, (0, 1, 2))
                if c == 1 and n == 9:
                    key_values(0, (3,))
                if c == 1 and n == 11:
                    attend(0)
                if c == 1 and n == 13:
                    turn_y(0)
                if c == 1 and n == 15:
                    film_out(0)
                if i + 3 < CHUNKS * N:
                    spread_b(i + 3)
            sum_states(CHUNKS * N - 1)
            out_proj(1)
            turn_x1(1)
            qkv(1)
            turn_qk(1)
            key_values(1, range(TILES))
            attend(1)
            turn_y(1)
            film_out(1)


def kernel(**inputs):
    import numpy as np
    import concourse.bacc as bacc
    from concourse.bass_utils import run_bass_kernel_spmd

    w = {name: np.ascontiguousarray(a) for name, a in inputs.items()}

    def slices(a):
        return np.ascontiguousarray(a.reshape(-1, P, a.shape[-1]).transpose(1, 0, 2)).reshape(P, -1)

    def column(a):
        return slices(a.reshape(-1, 1))

    def high(a):
        return np.concatenate([a, np.zeros((P - a.shape[0], a.shape[1]), a.dtype)])

    eye = np.eye(P, dtype=np.float32)
    xp = w["L0_cond_x_proj_w"].T
    parts = {
        "cond": slices(w["cond_2048"].T), "ada_w": slices(w["L0_cond_ada_w"].T), "ada_b": column(w["L0_cond_ada_b"]),
        "ln_g": column(w["L0_cond_ln_g"]), "ln_b": column(w["L0_cond_ln_b"]),
        "ident": eye, "in_w": w["L0_cond_in_proj_w"].T, "conv_w": slices(w["L0_cond_conv_w"]),
        "conv_b": column(w["L0_cond_conv_b"]), "xp_dt": slices(xp[:, :R]),
        "xp_bc": slices(np.concatenate([xp[:, R:]] * PARTS, axis=1)), "dt_w": high(w["L0_cond_dt_proj_w"].T),
        "dt_b": column(w["L0_cond_dt_proj_b"]), "a_log": slices(w["L0_cond_A_log"]),
        "d_skip": column(w["L0_cond_D_param"]),
        "sel_seed": high(np.concatenate([np.eye(BCR, dtype=np.float32)] * PARTS)),
        "out_w": slices(w["L0_cond_out_proj_w"].T), "norm_s": column(w["L1_cond_norm_scale"]),
        "norm_b": column(w["L1_cond_norm_bias"]), "wq": w["L1_cond_Wq"], "wk": w["L1_cond_Wk"], "wv": w["L1_cond_Wv"],
        "film_w": slices(w["L1_cond_film_emb_W"]), "film_b": column(w["L1_cond_film_emb_b"]),
        "fnorm_s": column(w["L1_cond_film_norm_scale"]), "fnorm_b": column(w["L1_cond_film_norm_bias"]),
        "fo_w": w["L1_cond_film_out_W"],
        "heads": np.kron(np.eye(D // HEAD, dtype=np.float32), np.ones((HEAD, HEAD), np.float32)),
    }

    def pack(names):
        return np.ascontiguousarray(np.concatenate([parts[name] for name, _ in names], axis=1))

    ones = np.ones((1, D), np.float32)
    mask = w["mask_BxS_ik0"]
    feeds = {
        "x": w["x"].reshape(B * S, D), "pack_ada": pack(PACK_ADA), "pack_ssm": pack(PACK_SSM), "pack_att": pack(PACK_ATT),
        "rows": np.concatenate([w["L1_cond_bq"][None], w["L1_cond_bv"][None], ones], axis=1),
        "key_rows": np.concatenate([ones, w["L1_cond_bk"][None]]),
        "mask_row": mask.reshape(1, B * S), "mask_tok": np.ascontiguousarray(mask.reshape(-1, P).T),
        "film_ob": w["L1_cond_film_out_b"],
    }
    nc = bacc.Bacc("TRN2", target_bir_lowering=False, num_devices=1)
    args = [nc.dram_tensor(f"in_{n}_dram", a.shape, mybir.dt.from_np(a.dtype), kind="ExternalInput").ap()
            for n, a in feeds.items()]
    out = nc.dram_tensor("out_0_dram", (B * S, D), mybir.dt.float32, kind="ExternalOutput").ap()
    mamba_attention_kernel(nc, *args, out)
    r = run_bass_kernel_spmd(nc, [{f"in_{n}_dram": a for n, a in feeds.items()}], core_ids=[0])
    return r.results[0]["out_0_dram"].reshape(B, S, D)
```

```python
import concourse.bass as bass
from concourse import mybir
from contextlib import ExitStack

B, S, D = 32, 32, 128
DI, N, R, CONV = 256, 16, 64, 4
HEAD = 8
E = 256
EPS = 1e-5
P = 128
HALVES = DI // P
CHUNKS = 2
CB_ = B // CHUNKS
CT = CB_ * S
TILES = CT // P
TB = P // S
KC = E // P
PARTS = 3
BCR = 2 * N
MASKED = -1e30

PACK_ADA = [("cond", KC * B), ("ada_w", KC * 3 * D), ("ada_b", 3), ("ln_g", 1), ("ln_b", 1)]
PACK_SSM = [("ident", P), ("in_w", 2 * DI), ("conv_w", HALVES * CONV), ("conv_b", HALVES), ("xp_dt", HALVES * R),
            ("xp_bc", HALVES * PARTS * BCR), ("dt_w", DI), ("dt_b", HALVES), ("a_log", HALVES * N),
            ("d_skip", HALVES), ("sel_seed", BCR)]
PACK_ATT = [("out_w", HALVES * D), ("norm_s", 1), ("norm_b", 1), ("wq", D), ("wk", D), ("wv", D),
            ("film_w", KC * 2 * D), ("film_b", 2), ("fnorm_s", 1), ("fnorm_b", 1), ("fo_w", D), ("heads", D)]


def columns(pack):
    at, out = 0, {}
    for name, width in pack:
        out[name] = (at, at + width)
        at += width
    return out, at


def mamba_attention_kernel(nc, x, pack_ada, pack_ssm, pack_att, rows, key_rows, mask_row, mask_tok, film_ob, out):
    fp32, bf16, i32 = mybir.dt.float32, mybir.dt.bfloat16, mybir.dt.int32
    ALU, ACT, AX = mybir.AluOpType, mybir.ActivationFunctionType, mybir.AxisListType

    with ExitStack() as ctx:
        def sb(name, shape, dt=fp32):
            return ctx.enter_context(nc.sbuf_tensor(name, shape, dt))

        def pb(name, shape):
            return ctx.enter_context(nc.psum_tensor(name, shape, fp32))

        def sem(name):
            return ctx.enter_context(nc.semaphore(name))

        x_sb = sb("x_sb", [P, CHUNKS * TILES, D])
        at_ada, n_ada = columns(PACK_ADA)
        at_ssm, n_ssm = columns(PACK_SSM)
        at_att, n_att = columns(PACK_ATT)
        ada_sb = sb("ada_sb", [P, n_ada])
        ssm_sb = sb("ssm_sb", [P, n_ssm])
        att_sb = sb("att_sb", [P, n_att])
        rows_sb = sb("rows_sb", [1, 3 * D])
        key_lhs = sb("key_lhs", [2, D])
        key_rhs = sb("key_rhs", [2, B * S])
        mask_row_i = sb("mask_row_i", [1, B * S], i32)
        mask_tok_i = sb("mask_tok_i", [P, CHUNKS * TILES], i32)
        film_ob_bc = sb("film_ob_bc", [P, D])

        def ada(name):
            return ada_sb[:, at_ada[name][0]:at_ada[name][1]]

        def ssm(name):
            return ssm_sb[:, at_ssm[name][0]:at_ssm[name][1]]

        def att(name):
            return att_sb[:, at_att[name][0]:at_att[name][1]]

        cond_in = ada("cond")
        ada_w = ada("ada_w").rearrange("p (k e) -> p k e", k=KC)
        ident = ssm("ident")
        in_w = ssm("in_w").rearrange("p (m e) -> p m e", e=P)
        conv_w = ssm("conv_w").rearrange("p (h k) -> p h k", h=HALVES)
        conv_b = ssm("conv_b")
        xp_dt = ssm("xp_dt").rearrange("p (h r) -> p h r", h=HALVES)
        xp_bc = ssm("xp_bc").rearrange("p (h r) -> p h r", h=HALVES)
        dt_w = ssm("dt_w")[0:R, :].rearrange("r (h d) -> r h d", h=HALVES)
        dt_b = ssm("dt_b")
        a_log = ssm("a_log")
        d_skip = ssm("d_skip")
        sel_seed = ssm("sel_seed")[0:PARTS * BCR, :]
        out_w = att("out_w").rearrange("p (h e) -> p h e", h=HALVES)
        film_w = att("film_w").rearrange("p (k e) -> p k e", k=KC)
        heads = att("heads")
        bq_row, bv_row, ones_row = (rows_sb[0:1, i * D:(i + 1) * D] for i in range(3))

        cond_s = sb("cond_s", [P, KC, B])
        adas = sb("adas", [P, 3, B])
        ln_tmp = sb("ln_tmp", [P, B])
        ln_mul = sb("ln_mul", [P, B])
        ln_add = sb("ln_add", [P, B])
        films = sb("films", [P, 2, B])
        film_tmp = sb("film_tmp", [P, B])
        film_mul = sb("film_mul", [P, B])
        film_add = sb("film_add", [P, B])
        gate_tok = sb("gate_tok", [P, CHUNKS * TILES, D])
        a_exp = sb("a_exp", [P, HALVES * N])
        a_neg = sb("a_neg", [P, HALVES * N])
        sel = sb("sel", [PARTS * BCR, BCR, P], bf16)
        diag_d = sb("diag_d", [P, HALVES, P])
        valid = sb("valid", [P, CHUNKS * TILES])
        half_neg = sb("half_neg", [P, TILES])

        def per_chunk(name, shape, dt=fp32):
            return [sb(f"{name}{c}", shape, dt) for c in range(CHUNKS)]

        def shared(name, shape, dt=fp32):
            return [sb(name, shape, dt)] * CHUNKS

        def norm_buffers(name):
            return {"stats": shared(name + "_stats", [P, TILES, 6]), "mv": shared(name + "_mv", [P, TILES, 2]),
                    "var": shared(name + "_var", [P, TILES]), "rstd": shared(name + "_rstd", [P, TILES]),
                    "hat": shared(name + "_hat", [P, TILES, D])}

        ln0, ln1, ln2 = norm_buffers("ln0"), norm_buffers("ln1"), norm_buffers("ln2")
        xn = shared("xn", [P, CT])
        u = per_chunk("u", [P, HALVES, CT])
        z_s = per_chunk("z_s", [P, HALVES, CT])
        bc_parts = per_chunk("bc_parts", [PARTS * BCR, CT], bf16)
        bc_rest = shared("bc_rest", [PARTS * BCR, CT])
        dt_r = shared("dt_r", [R, CT])
        sp = shared("sp", [P, HALVES, CT])
        dt = per_chunk("dt", [P, HALVES, CT])
        dtu = per_chunk("dtu", [P, HALVES, CT])
        g = shared("g", [P, HALVES, CT])
        x1 = shared("x1", [P, TILES, D])
        x1b = shared("x1b", [P, TILES, D])
        x1n = shared("x1n", [P, CT])
        k_max = shared("k_max", [P, CB_])
        k_exp = shared("k_exp", [P, CT])
        k_sum = shared("k_sum", [P, CB_])
        k_den = shared("k_den", [P, CB_])
        k_inv = shared("k_inv", [P, CB_])
        k_soft = shared("k_soft", [P, CT])
        q_max = shared("q_max", [P, TILES * D // HEAD])
        q_exp = shared("q_exp", [P, TILES * D])
        q_sum = shared("q_sum", [P, TILES * D // HEAD])
        q_inv = shared("q_inv", [P, TILES * D // HEAD])
        v_sb = shared("v_sb", [P, TILES, D])
        q_cm = shared("q_cm", [P, CT])
        k_big = sb("k_big", [P, TILES, TB, D])
        kv = sb("kv", [P, TILES, TB, D])
        gate_x = kv[:, 0:2, :, :].rearrange("p t j e -> p (t j e)")
        y1 = shared("y1", [P, TILES, D])
        fh = shared("fh", [P, CT])
        res = per_chunk("res", [P, TILES, D])

        RD, RB, RH, RC = 4, 5, 3, 3
        LEAD = 2
        decay = sb("decay", [P, RD, HALVES, CT])
        b_bc = sb("b_bc", [P, RB, CT])
        drive = sb("drive", [P, RD, HALVES, CT])
        state = sb("state", [P, RH, HALVES, CT])
        hc = sb("hc", [P, RC, HALVES, CT])

        y_ps = [pb(f"y_ps{h}", [P, CT]) for h in range(HALVES)]
        c_ps = [pb(f"c_ps{i}", [P, CT]) for i in range(2)]
        b_ps = pb("b_ps", [P, CT])
        w0, w1, w2 = (pb(f"w{i}", [P, CT]) for i in range(3))

        att_banks = [
            {"proj": w0, "x1T": w1, "k": w2, "q": w0, "v": w1, "qT": w0, "kT": w2, "kv": (w1, w2, w0, w1), "y1": w2,
             "yT": w0, "out": w1},
            {"proj": w0, "x1T": w1, "k": c_ps[0], "q": c_ps[1], "v": b_ps, "qT": w2, "kT": y_ps[0],
             "kv": (y_ps[1], w0, w1, c_ps[0]), "y1": c_ps[1], "yT": b_ps, "out": w2},
        ]

        x_in = [sem(f"x_in{c}") for c in range(CHUNKS)]
        ada_in, ssm_in, att_in, row_in, mask_in, out_done = (
            sem(n) for n in ("ada_in", "ssm_in", "att_in", "row_in", "mask_in", "out_done"))
        names = """cleared const_gp cond_ready ada_mm ada_biased ln_tmp_ready ln_affine gate_spread gate_mm gate_ready mask_neg film_mm
            film_biased film_affine a_exp_ready a_ready mask_ready
            stat0 aggr0 var0 rstd0 hat0 hat0_T xg_ready xn_ready x_mm z_mm conv_first conv_tap u_ready z_ready
            bc_mm bc_top bc_rest_ready bc_mid bc_ready dtr_mm dtr_ready dt_mm sp_abs sp_relu sp_exp_ready sp_ready dt_ready
            dtu_ready b_mm b_copied drive_ready decay_ready scan_done c_mm hc_ready y_mm
            g_ready proj_mm gated_ready x1_ready x1b_ready stat1 aggr1 var1 rstd1 hat1 hat1_T x1n_ready
            k_mm k_max_ready k_sub_ready k_exp_ready k_sum_ready k_den_ready k_inv_ready k_soft_ready
            q_mm q_max_ready q_sub_ready q_exp_ready q_sum_ready q_inv_ready v_mm v_ready
            q_T q_cm_ready k_T k_big_ready kv_mm kv_ready y1_mm y1_ready
            stat2 aggr2 var2 rstd2 hat2 hat2_T fm_ready fh_ready fs_ready fo_mm res_ready""".split()
        s = {name: sem(name) for name in names}

        def batches(ap):
            return ap.rearrange("p (b t) -> p b t", t=S)

        def over_steps(ap):
            return ap.unsqueeze(2).broadcast_to([P, CB_, S])

        def over_head(ap):
            return ap.unsqueeze(2).broadcast_to([P, TILES * D // HEAD, HEAD])

        def in_heads(ap):
            return ap.rearrange("p (g e) -> p g e", e=HEAD)

        def mine(c):
            return slice(c * CB_, (c + 1) * CB_)

        def tiled(ap):
            return ap.rearrange("p (t e) -> p t e", e=D)

        block = ctx.enter_context(nc.Block())

        @block.sync
        def _(sync):
            x_v = x.rearrange("(n p) d -> p n d", p=P)
            sync.dma_start(x_sb[:, 0:TILES, :], x_v[:, 0:TILES, :]).then_inc(x_in[0], 16)
            sync.dma_start(ssm_sb[:, :], pack_ssm).then_inc(ssm_in, 16)
            sync.dma_start(x_sb[:, TILES:, :], x_v[:, TILES:, :]).then_inc(x_in[1], 16)
            sync.dma_start(mask_row_i[:, :], mask_row).then_inc(mask_in, 16)
            sync.dma_start(mask_tok_i[:, :], mask_tok).then_inc(mask_in, 16)
            out_v = out.rearrange("(n p) d -> p n d", p=P)
            for c in range(CHUNKS):
                sync.wait_ge(s["res_ready"], c + 1)
                sync.dma_start(out_v[:, c * TILES:(c + 1) * TILES, :], res[c][:, :, :]).then_inc(out_done, 16)
            sync.wait_ge(out_done, 16 * CHUNKS)

        @block.gpsimd
        def _(gp):
            tt, ts = nc.gpsimd.tensor_tensor, nc.gpsimd.tensor_scalar

            def rstd(k, buf, c):
                gp.wait_ge(s[f"var{k}"], c + 1)
                if k == 0 and c == 0:
                    gp.wait_ge(s["cleared"], 4)
                tt(buf["rstd"][c][:, :], buf["var"][c][:, :], half_neg[:, :], ALU.pow).then_inc(s[f"rstd{k}"], 1)

            def drive_step(i):
                c = i // N
                if i % N == 0:
                    gp.wait_ge(s["dtu_ready"], HALVES * (c + 1))
                gp.wait_ge(s["b_copied"], i + 1)
                if i >= RD:
                    gp.wait_ge(s["scan_done"], i - RD + 1)
                tt(drive[:, i % RD, :, :], dtu[c][:, :, :],
                   b_bc[:, i % RB, :].unsqueeze(1).broadcast_to([P, HALVES, CT]), ALU.mult).then_inc(s["drive_ready"], 1)

            nc.gpsimd.memset(half_neg[:, :], -0.5).then_inc(s["cleared"], 1)
            nc.gpsimd.memset(decay[:, :, :, :].rearrange("p r h (b t) -> p (r h b) t", t=S)[:, :, 0:1], 0.0)\
                .then_inc(s["cleared"], 1)
            nc.gpsimd.memset(key_rhs[:, :], 1.0).then_inc(s["cleared"], 1)
            nc.gpsimd.memset(k_big[:, :, :, :], 0.0).then_inc(s["cleared"], 1)
            rstd(0, ln0, 0)
            gp.wait_ge(ssm_in, 16)
            ts(sel[:, :, :], sel_seed.unsqueeze(2).broadcast_to([PARTS * BCR, BCR, P]), 1.0, 0.0, ALU.mult, ALU.add)\
                .then_inc(s["const_gp"], 1)
            for h in range(HALVES):
                ts(diag_d[:, h, :], ident, d_skip[:, h:h + 1], 0.0, ALU.mult, ALU.add).then_inc(s["const_gp"], 1)

            def late_sums(c):
                gp.wait_ge(s["x1_ready"], c + 1)
                gp.wait_ge(row_in, 48)
                tt(x1b[c][:, :, :], x1[c][:, :, :], film_ob_bc[:, :].unsqueeze(1).broadcast_to([P, TILES, D]),
                   ALU.add).then_inc(s["x1b_ready"], 1)

            def adaptive_shift(c):
                gp.wait_ge(s["xg_ready"], c + 1)
                gp.wait_ge(s["ln_affine"], 2)
                tt(batches(xn[c][:, :]), batches(xn[c][:, :]), over_steps(ln_add[:, mine(c)]), ALU.add)\
                    .then_inc(s["xn_ready"], 1)

            def film_shift(c):
                gp.wait_ge(s["fm_ready"], c + 1)
                gp.wait_ge(s["film_affine"], 3)
                tt(batches(fh[c][:, :]), batches(fh[c][:, :]), over_steps(film_add[:, mine(c)]), ALU.add)\
                    .then_inc(s["fh_ready"], 1)

            def soft_keys(c):
                gp.wait_ge(s["k_inv_ready"], c + 1)
                tt(batches(k_soft[c][:, :]), batches(k_exp[c][:, :]), over_steps(k_inv[c][:, :]), ALU.mult)\
                    .then_inc(s["k_soft_ready"], 1)

            gp.wait_ge(s["ada_biased"], 1)
            ts(gate_x.rearrange("p (b t) -> p b t", t=S), adas[:, 2, :].unsqueeze(2).broadcast_to([P, B, S]), 1.0, 0.0,
               ALU.mult, ALU.add).then_inc(s["gate_spread"], 1)
            gp.dma_start(rows_sb[:, :], rows).then_inc(row_in, 16)
            gp.dma_start(key_lhs[:, :], key_rows).then_inc(row_in, 16)
            gp.dma_start(film_ob_bc[:, :], film_ob.partition_broadcast(P)).then_inc(row_in, 16)
            gp.wait_ge(mask_in, 32)
            ts(key_rhs[0:1, :], mask_row_i[:, :], 1.0, MASKED, ALU.is_equal, ALU.mult).then_inc(s["mask_ready"], 1)
            ts(valid[:, :], mask_tok_i[:, :], 1.0, -1.0, ALU.is_equal, ALU.mult).then_inc(s["mask_neg"], 1)
            gp.wait_ge(s["mask_neg"], 1)
            ts(valid[:, :], valid[:, :], 1.0, 1.0, ALU.mult, ALU.add).then_inc(s["mask_ready"], 1)
            rstd(0, ln0, 1)
            for i in range(LEAD):
                drive_step(i)
            for i in range(CHUNKS * N):
                c, n = i // N, i % N
                if i + LEAD < CHUNKS * N:
                    drive_step(i + LEAD)
                if c == 0 and n == 1:
                    adaptive_shift(1)
                if c == 1 and n == 3:
                    rstd(1, ln1, 0)
                if c == 1 and n == 8:
                    soft_keys(0)
                if c == 1 and n == 9:
                    late_sums(0)
                if c == 1 and n == 13:
                    rstd(2, ln2, 0)
                if c == 1 and n == 15:
                    film_shift(0)
            rstd(1, ln1, 1)
            late_sums(1)
            rstd(2, ln2, 1)

        @block.scalar
        def _(act):
            A = nc.scalar.activation
            act.dma_start(ada_sb[:, :], pack_ada).then_inc(ada_in, 16)
            act.dma_start(att_sb[:, :], pack_att).then_inc(att_in, 16)

            act.wait_ge(ada_in, 16)
            A(cond_s[:, :, :].rearrange("p k b -> p (k b)"), cond_in, ACT.Silu).then_inc(s["cond_ready"], 1)

            def conv_start(c):
                for h, bank in enumerate((w1, w2)):
                    act.wait_ge(s["x_mm"], HALVES * c + h + 1)
                    A(u[c][:, h, :], bank[:, :], ACT.Identity, bias=conv_b[:, h:h + 1],
                      scale=conv_w[:, h, CONV - 1:CONV]).then_inc(s["conv_first"], 1)

            def silu_u(c):
                for h in range(HALVES):
                    act.wait_ge(s["conv_tap"], HALVES * (CONV - 1) * c + HALVES * (CONV - 2) + h + 1)
                    A(u[c][:, h, :], u[c][:, h, :], ACT.Silu).then_inc(s["u_ready"], 1)

            def silu_z(c, banks):
                for h, bank in enumerate(banks):
                    act.wait_ge(s["z_mm"], HALVES * c + h + 1)
                    A(z_s[c][:, h, :], bank[:, :], ACT.Silu).then_inc(s["z_ready"], 1)

            def copy_dt_rows(c):
                act.wait_ge(s["dtr_mm"], c + 1)
                A(dt_r[c][:, :], w0[0:R, :], ACT.Copy).then_inc(s["dtr_ready"], 1)

            def top_bc(c):
                act.wait_ge(s["bc_mm"], c + 1)
                A(bc_parts[c][:, :], w0[0:PARTS * BCR, :], ACT.Copy).then_inc(s["bc_top"], 1)

            def copy_gates():
                for c in range(CHUNKS):
                    act.wait_ge(s["gate_mm"], c + 1)
                    A(gate_tok[:, c * TILES:(c + 1) * TILES, :], tiled(c_ps[c][:, :]), ACT.Copy)\
                        .then_inc(s["gate_ready"], 1)

            def softplus(c):
                for h, bank in enumerate((w1, w2)):
                    act.wait_ge(s["dt_mm"], HALVES * c + h + 1)
                    A(sp[c][:, h, :], bank[:, :], ACT.Abs, bias=dt_b[:, h:h + 1]).then_inc(s["sp_abs"], 1)
                    if c:
                        A(dt[c][:, h, :], bank[:, :], ACT.Relu, bias=dt_b[:, h:h + 1]).then_inc(s["sp_relu"], 1)
                act.wait_ge(s["sp_abs"], HALVES * (c + 1))

            def softplus_end(c):
                for h in range(HALVES):
                    A(sp[c][:, h, :], sp[c][:, h, :], ACT.Exp, scale=-1.0).then_inc(s["sp_exp_ready"], 1)
                for h in range(HALVES):
                    act.wait_ge(s["sp_exp_ready"], HALVES * c + h + 1)
                    A(sp[c][:, h, :], sp[c][:, h, :], ACT.Ln, bias=1.0).then_inc(s["sp_ready"], 1)

            def decays(i):
                c, n = i // N, i % N
                if n == 0:
                    act.wait_ge(s["dt_ready"], HALVES * (c + 1))
                    act.wait_ge(s["a_ready"], 1)
                    act.wait_ge(s["cleared"], 2)
                if i >= RD:
                    act.wait_ge(s["scan_done"], i - RD + 1)
                for h in range(HALVES):
                    A(batches(decay[:, i % RD, h, :])[:, :, 1:S], batches(dt[c][:, h, :])[:, :, 1:S], ACT.Exp,
                      scale=a_neg[:, h * N + n:h * N + n + 1]).then_inc(s["decay_ready"], 1)

            def copy_b(i):
                act.wait_ge(s["b_mm"], i + 1)
                if i >= RB:
                    act.wait_ge(s["drive_ready"], i - RB + 1)
                A(b_bc[:, i % RB, :], b_ps[:, :], ACT.Copy).then_inc(s["b_copied"], 1)

            def x1_affine(c):
                act.wait_ge(s["hat1_T"], c + 1)
                if c == 0:
                    act.wait_ge(att_in, 16)
                A(x1n[c][:, :], att_banks[c]["x1T"][:, :], ACT.Identity, bias=att("norm_b"), scale=att("norm_s"))\
                    .then_inc(s["x1n_ready"], 1)

            def values(c):
                act.wait_ge(s["v_mm"], c + 1)
                for t in range(TILES):
                    A(v_sb[c][:, t, :], tiled(att_banks[c]["v"][:, :])[:, t, :], ACT.Copy, scale=valid[:, c * TILES + t:c * TILES + t + 1])\
                        .then_inc(s["v_ready"], 1)

            def key_exp(c):
                act.wait_ge(s["k_sub_ready"], c + 1)
                A(k_exp[c][:, :], k_exp[c][:, :], ACT.Exp).then_inc(s["k_exp_ready"], 1)

            def query_exp(c):
                act.wait_ge(s["q_sub_ready"], c + 1)
                A(q_exp[c][:, :], q_exp[c][:, :], ACT.Exp).then_inc(s["q_exp_ready"], 1)

            def copy_q(c):
                act.wait_ge(s["q_T"], c + 1)
                A(q_cm[c][:, :], att_banks[c]["qT"][:, :], ACT.Copy).then_inc(s["q_cm_ready"], 1)

            def turned(c):
                if c == 0:
                    copy_q(c)
                act.wait_ge(s["k_T"], c + 1)
                act.wait_ge(s["cleared"], 4)
                if c:
                    act.wait_ge(s["kv_mm"], TILES * c)
                for j in range(TB if c == 0 else TB // 2):
                    A(k_big[j * S:(j + 1) * S, :, j, :], tiled(att_banks[c]["kT"][j * S:(j + 1) * S, :]), ACT.Copy)\
                        .then_inc(s["k_big_ready"], 1)

            def film_silu(c):
                act.wait_ge(s["fh_ready"], c + 1)
                A(fh[c][:, :], fh[c][:, :], ACT.Silu).then_inc(s["fs_ready"], 1)

            conv_start(0)
            silu_z(0, y_ps)
            copy_gates()
            silu_u(0)
            copy_dt_rows(0)
            nc.scalar.preload_act_table_set("natural_log_exp_and_others")
            A(a_exp[:, :], a_log, ACT.Exp).then_inc(s["a_exp_ready"], 1)
            softplus(0)
            top_bc(0)
            softplus_end(0)
            for i in range(3):
                copy_b(i)
                if i < LEAD:
                    decays(i)
            for i in range(CHUNKS * N):
                c, n = i // N, i % N
                if i + LEAD < CHUNKS * N:
                    decays(i + LEAD)
                if i + 3 < CHUNKS * N:
                    copy_b(i + 3)
                if c == 0 and n == 3:
                    conv_start(1)
                if c == 0 and n == 7:
                    silu_u(1)
                    silu_z(1, (w0, w1))
                    nc.scalar.preload_act_table_set("natural_log_exp_and_others")
                if c == 0 and n == 8:
                    copy_dt_rows(1)
                if c == 0 and n == 9:
                    softplus(1)
                if c == 0 and n == 10:
                    top_bc(1)
                    softplus_end(1)
                if c == 1 and n == 4:
                    x1_affine(0)
                if c == 1 and n == 7:
                    key_exp(0)
                if c == 1 and n == 8:
                    query_exp(0)
                    values(0)
                if c == 1 and n == 9:
                    turned(0)
                if c == 1 and n == 15:
                    film_silu(0)
                    nc.scalar.preload_act_table_set("natural_log_exp_and_others")
            x1_affine(1)
            key_exp(1)
            query_exp(1)
            values(1)
            turned(1)
            copy_q(1)
            film_silu(1)

        @block.vector
        def _(dve):
            V = nc.vector

            def norm_stats(k, buf, c, src):
                if k:
                    dve.wait_ge(s[("", "x1_ready", "y1_ready")[k]], c + 1)
                for t in range(TILES):
                    V.bn_stats(buf["stats"][c][:, t, :], src(t)).then_inc(s[f"stat{k}"], 1)
                dve.wait_ge(s[f"stat{k}"], TILES * (c + 1))
                for t in range(TILES):
                    V.bn_aggr(buf["mv"][c][:, t, :], buf["stats"][c][:, t, :]).then_inc(s[f"aggr{k}"], 1)
                dve.wait_ge(s[f"aggr{k}"], TILES * (c + 1))
                V.tensor_scalar(buf["var"][c][:, :], buf["mv"][c][:, :, 1:2].rearrange("p t o -> p (t o)"), EPS, None,
                                ALU.add).then_inc(s[f"var{k}"], 1)

            def normalise(k, buf, c, src):
                dve.wait_ge(s[f"rstd{k}"], c + 1)
                for t in range(TILES):
                    V.tensor_scalar(buf["hat"][c][:, t, :], src(t), buf["mv"][c][:, t, 0:1], buf["rstd"][c][:, t:t + 1],
                                    ALU.subtract, ALU.mult).then_inc(s[f"hat{k}"], 1)

            def x_tile(c):
                return lambda t: x_sb[:, c * TILES + t, :]

            def adaptive(c):
                dve.wait_ge(s["hat0_T"], c + 1)
                V.tensor_tensor(batches(xn[c][:, :]), batches(w0[:, :]), over_steps(ln_mul[:, mine(c)]), ALU.mult)\
                    .then_inc(s["xg_ready"], 1)
                if c == 0:
                    dve.wait_ge(s["xg_ready"], c + 1)
                    V.tensor_tensor(batches(xn[c][:, :]), batches(xn[c][:, :]), over_steps(ln_add[:, mine(c)]), ALU.add)\
                        .then_inc(s["xn_ready"], 1)

            def conv_taps(c, backs=range(1, CONV)):
                for back in backs:
                    for h, bank in enumerate((w1, w2)):
                        if back == 1:
                            dve.wait_ge(s["conv_first"], HALVES * c + h + 1)
                        else:
                            dve.wait_ge(s["conv_tap"], HALVES * ((CONV - 1) * c + back - 2) + h + 1)
                        V.scalar_tensor_tensor(
                            out=batches(u[c][:, h, :])[:, :, back:S], in0=batches(bank[:, :])[:, :, 0:S - back],
                            scalar=conv_w[:, h, CONV - 1 - back:CONV - back],
                            in1=batches(u[c][:, h, :])[:, :, back:S], op0=ALU.mult, op1=ALU.add)\
                            .then_inc(s["conv_tap"], 1)

            def rest_bc(c):
                dve.wait_ge(s["bc_top"], c + 1)
                V.tensor_tensor(bc_rest[c][:, :], w0[0:PARTS * BCR, :], bc_parts[c][:, :], ALU.subtract)\
                    .then_inc(s["bc_rest_ready"], 1)

            def split_bc(c):
                dve.wait_ge(s["bc_rest_ready"], c + 1)
                for part in range(1, PARTS):
                    r = slice(part * BCR, (part + 1) * BCR)
                    V.tensor_copy(bc_parts[c][r, :], bc_rest[c][r, :]).then_inc(s["bc_mid"], 1)
                dve.wait_ge(s["bc_mid"], 2 * (c + 1))
                V.tensor_tensor(bc_parts[c][r, :], bc_rest[c][r, :], bc_parts[c][r, :], ALU.subtract)\
                    .then_inc(s["bc_ready"], 1)

            def relu_dt(c):
                for h, bank in enumerate((w1, w2)):
                    dve.wait_ge(s["sp_abs"], HALVES * c + h + 1)
                    V.tensor_scalar(dt[c][:, h, :], bank[:, :], dt_b[:, h:h + 1], 0.0, ALU.add, ALU.max)\
                        .then_inc(s["sp_relu"], 1)

            def steps_dt(c):
                dve.wait_ge(s["sp_relu"], HALVES * (c + 1))
                for h in range(HALVES):
                    dve.wait_ge(s["sp_ready"], HALVES * c + h + 1)
                    V.tensor_tensor(dt[c][:, h, :], sp[c][:, h, :], dt[c][:, h, :], ALU.add).then_inc(s["dt_ready"], 1)

            def steps_dtu(c):
                dve.wait_ge(s["u_ready"], HALVES * (c + 1))
                for h in range(HALVES):
                    dve.wait_ge(s["dt_ready"], HALVES * c + h + 1)
                    V.tensor_tensor(dtu[c][:, h, :], dt[c][:, h, :], u[c][:, h, :], ALU.mult).then_inc(s["dtu_ready"], 1)

            def scan(i):
                dve.wait_ge(s["decay_ready"], HALVES * (i + 1))
                dve.wait_ge(s["drive_ready"], i + 1)
                if i >= RH:
                    dve.wait_ge(s["hc_ready"], i - RH + 1)
                V.tensor_tensor_scan(state[:, i % RH, :, :].rearrange("p h t -> p (h t)"),
                                     decay[:, i % RD, :, :].rearrange("p h t -> p (h t)"),
                                     drive[:, i % RD, :, :].rearrange("p h t -> p (h t)"),
                                     0.0, ALU.mult, ALU.add).then_inc(s["scan_done"], 1)

            def weigh(i):
                dve.wait_ge(s["scan_done"], i + 1)
                dve.wait_ge(s["c_mm"], i + 1)
                if i >= RC:
                    dve.wait_ge(s["y_mm"], i - RC + 1)
                V.tensor_tensor(hc[:, i % RC, :, :], state[:, i % RH, :, :],
                                c_ps[i % 2][:, :].unsqueeze(1).broadcast_to([P, HALVES, CT]), ALU.mult)\
                    .then_inc(s["hc_ready"], 1)

            def gate_z(c):
                dve.wait_ge(s["y_mm"], N * (c + 1))
                dve.wait_ge(s["z_ready"], HALVES * (c + 1))
                for h in range(HALVES):
                    V.tensor_tensor(g[c][:, h, :], y_ps[h][:, :], z_s[c][:, h, :], ALU.mult).then_inc(s["g_ready"], 1)

            def residual(c):
                dve.wait_ge(s["proj_mm"], c + 1)
                dve.wait_ge(s["gate_ready"], 2)
                V.tensor_tensor(x1[c][:, :, :], tiled(att_banks[c]["proj"][:, :]), gate_tok[:, c * TILES:(c + 1) * TILES, :], ALU.mult)\
                    .then_inc(s["gated_ready"], 1)
                dve.wait_ge(s["gated_ready"], c + 1)
                V.tensor_tensor(x1[c][:, :, :], x1[c][:, :, :], x_sb[:, c * TILES:(c + 1) * TILES, :], ALU.add)\
                    .then_inc(s["x1_ready"], 1)

            def keys(c):
                dve.wait_ge(s["k_mm"], c + 1)
                V.tensor_reduce(k_max[c][:, :], batches(att_banks[c]["k"][:, :]), op=ALU.max, axis=AX.X).then_inc(s["k_max_ready"], 1)
                dve.wait_ge(s["k_max_ready"], c + 1)
                V.tensor_tensor(batches(k_exp[c][:, :]), batches(att_banks[c]["k"][:, :]), over_steps(k_max[c][:, :]), ALU.subtract)\
                    .then_inc(s["k_sub_ready"], 1)

            def queries(c):
                dve.wait_ge(s["q_mm"], c + 1)
                V.tensor_reduce(q_max[c][:, :], in_heads(att_banks[c]["q"][:, :]), op=ALU.max, axis=AX.X).then_inc(s["q_max_ready"], 1)
                dve.wait_ge(s["q_max_ready"], c + 1)
                V.tensor_tensor(in_heads(q_exp[c][:, :]), in_heads(att_banks[c]["q"][:, :]), over_head(q_max[c][:, :]), ALU.subtract)\
                    .then_inc(s["q_sub_ready"], 1)

            def key_sums(c):
                dve.wait_ge(s["k_exp_ready"], c + 1)
                V.tensor_reduce(k_sum[c][:, :], batches(k_exp[c][:, :]), op=ALU.add, axis=AX.X).then_inc(s["k_sum_ready"], 1)
                dve.wait_ge(s["k_sum_ready"], c + 1)
                V.scalar_tensor_tensor(out=k_den[c][:, :], in0=k_max[c][:, :], scalar=MASKED / 2, in1=k_sum[c][:, :],
                                       op0=ALU.is_ge, op1=ALU.mult).then_inc(s["k_den_ready"], 1)
                dve.wait_ge(s["k_den_ready"], c + 1)
                V.reciprocal(k_inv[c][:, :], k_den[c][:, :]).then_inc(s["k_inv_ready"], 1)

            def soft_keys(c):
                dve.wait_ge(s["k_inv_ready"], c + 1)
                V.tensor_tensor(batches(k_soft[c][:, :]), batches(k_exp[c][:, :]), over_steps(k_inv[c][:, :]), ALU.mult)\
                    .then_inc(s["k_soft_ready"], 1)

            def spread_keys(c, js):
                dve.wait_ge(s["k_T"], c + 1)
                dve.wait_ge(s["kv_mm"], TILES * c)
                for j in js:
                    V.tensor_copy(k_big[j * S:(j + 1) * S, :, j, :], tiled(att_banks[c]["kT"][j * S:(j + 1) * S, :]))\
                        .then_inc(s["k_big_ready"], 1)

            def query_sums(c):
                dve.wait_ge(s["q_exp_ready"], c + 1)
                V.tensor_reduce(q_sum[c][:, :], in_heads(q_exp[c][:, :]), op=ALU.add, axis=AX.X)\
                    .then_inc(s["q_sum_ready"], 1)
                dve.wait_ge(s["q_sum_ready"], c + 1)
                V.reciprocal(q_inv[c][:, :], q_sum[c][:, :]).then_inc(s["q_inv_ready"], 1)

            def head_blocks(c, tiles):
                if c:
                    dve.wait_ge(s["y1_mm"], c)
                for t in tiles:
                    bank = att_banks[c]["kv"][t]
                    dve.wait_ge(s["kv_mm"], TILES * c + t + 1)
                    V.tensor_tensor(kv[:, t, :, :], tiled(bank[:, :]), heads.unsqueeze(1).broadcast_to([P, TB, D]),
                                    ALU.mult).then_inc(s["kv_ready"], 1)

            def attended(c):
                dve.wait_ge(s["y1_mm"], c + 1)
                dve.wait_ge(s["q_inv_ready"], c + 1)
                V.tensor_tensor(in_heads(y1[c][:, :, :].rearrange("p t e -> p (t e)")), in_heads(att_banks[c]["y1"][:, :]),
                                over_head(q_inv[c][:, :]), ALU.mult).then_inc(s["y1_ready"], 1)

            def film(c):
                dve.wait_ge(s["hat2_T"], c + 1)
                V.tensor_tensor(batches(fh[c][:, :]), batches(att_banks[c]["yT"][:, :]), over_steps(film_mul[:, mine(c)]), ALU.mult)\
                    .then_inc(s["fm_ready"], 1)
                if c:
                    dve.wait_ge(s["fm_ready"], c + 1)
                    V.tensor_tensor(batches(fh[c][:, :]), batches(fh[c][:, :]), over_steps(film_add[:, mine(c)]), ALU.add)\
                        .then_inc(s["fh_ready"], 1)

            def finish(c):
                dve.wait_ge(s["fo_mm"], c + 1)
                dve.wait_ge(s["x1b_ready"], c + 1)
                V.tensor_tensor(res[c][:, :, :], tiled(att_banks[c]["out"][:, :]), x1b[c][:, :, :], ALU.add).then_inc(s["res_ready"], 1)

            dve.wait_ge(x_in[0], 16)
            norm_stats(0, ln0, 0, x_tile(0))
            normalise(0, ln0, 0, x_tile(0))
            dve.wait_ge(s["ada_mm"], 1)
            V.tensor_tensor(adas[:, :, :], w1[:, 0:3 * B].rearrange("p (m b) -> p m b", b=B),
                            ada("ada_b").unsqueeze(2).broadcast_to([P, 3, B]), ALU.add).then_inc(s["ada_biased"], 1)
            dve.wait_ge(s["ada_biased"], 1)
            V.tensor_scalar(ln_tmp[:, :], adas[:, 1, :], 1.0, ada("ln_b"), ALU.add, ALU.mult).then_inc(s["ln_tmp_ready"], 1)
            V.tensor_scalar(ln_mul[:, :], adas[:, 1, :], 1.0, ada("ln_g"), ALU.add, ALU.mult).then_inc(s["ln_affine"], 1)
            dve.wait_ge(s["ln_tmp_ready"], 1)
            V.tensor_tensor(ln_add[:, :], ln_tmp[:, :], adas[:, 0, :], ALU.add).then_inc(s["ln_affine"], 1)
            dve.wait_ge(s["ln_affine"], 2)
            adaptive(0)
            conv_taps(0)
            dve.wait_ge(x_in[1], 16)
            dve.wait_ge(s["hat0_T"], 1)
            norm_stats(0, ln0, 1, x_tile(1))
            normalise(0, ln0, 1, x_tile(1))
            dve.wait_ge(s["a_exp_ready"], 1)
            V.tensor_scalar(a_neg[:, :], a_exp[:, :], -1.0, None, ALU.mult).then_inc(s["a_ready"], 1)
            relu_dt(0)
            rest_bc(0)
            split_bc(0)
            steps_dt(0)
            steps_dtu(0)

            def film_constants():
                dve.wait_ge(s["film_mm"], 1)
                V.tensor_tensor(films[:, :, :], w1[:, 0:2 * B].rearrange("p (m b) -> p m b", b=B),
                                att("film_b").unsqueeze(2).broadcast_to([P, 2, B]), ALU.add).then_inc(s["film_biased"], 1)
                dve.wait_ge(s["film_biased"], 1)
                V.tensor_scalar(film_mul[:, :], films[:, 0, :], 1.0, att("fnorm_s"), ALU.add, ALU.mult)\
                    .then_inc(s["film_affine"], 1)
                V.tensor_scalar(film_tmp[:, :], films[:, 0, :], 1.0, att("fnorm_b"), ALU.add, ALU.mult)\
                    .then_inc(s["film_affine"], 1)
                dve.wait_ge(s["film_affine"], 2)
                V.tensor_tensor(film_add[:, :], film_tmp[:, :], films[:, 1, :], ALU.add).then_inc(s["film_affine"], 1)

            for i in range(CHUNKS * N):
                c, n = i // N, i % N
                scan(i)
                if i > 0:
                    weigh(i - 1)
                if c == 0 and n == 1:
                    adaptive(1)
                if c == 0 and 4 <= n < 4 + CONV - 1:
                    conv_taps(1, (n - 3,))
                if c == 0 and n == 14:
                    film_constants()
                if c == 0 and n == 11:
                    rest_bc(1)
                    split_bc(1)
                if c == 0 and n == 12:
                    steps_dt(1)
                if c == 0 and n == 13:
                    steps_dtu(1)
                if c == 1 and n == 1:
                    gate_z(0)
                if c == 1 and n == 2:
                    residual(0)
                if c == 1 and n == 3:
                    norm_stats(1, ln1, 0, lambda t: x1[0][:, t, :])
                if c == 1 and n == 4:
                    normalise(1, ln1, 0, lambda t: x1[0][:, t, :])
                if c == 1 and n == 7:
                    keys(0)
                if c == 1 and n == 8:
                    queries(0)
                    key_sums(0)
                if c == 1 and n == 9:
                    query_sums(0)
                if c == 1 and n == 11:
                    head_blocks(0, (0, 1))
                if c == 1 and n == 12:
                    head_blocks(0, (2, 3))
                if c == 1 and n == 13:
                    attended(0)
                    norm_stats(2, ln2, 0, lambda t: y1[0][:, t, :])
                if c == 1 and n == 14:
                    normalise(2, ln2, 0, lambda t: y1[0][:, t, :])
                if c == 1 and n == 15:
                    film(0)
            weigh(CHUNKS * N - 1)
            gate_z(1)
            finish(0)
            residual(1)
            norm_stats(1, ln1, 1, lambda t: x1[1][:, t, :])
            normalise(1, ln1, 1, lambda t: x1[1][:, t, :])
            keys(1)
            queries(1)
            key_sums(1)
            soft_keys(1)
            query_sums(1)
            spread_keys(1, range(TB // 2, TB))
            head_blocks(1, range(TILES))
            attended(1)
            norm_stats(2, ln2, 1, lambda t: y1[1][:, t, :])
            normalise(2, ln2, 1, lambda t: y1[1][:, t, :])
            film(1)
            finish(1)

        @block.tensor
        def _(pe):
            mm = nc.tensor.matmul

            def turn(bank, src, done, ready=None, before=0):
                for t in range(TILES):
                    if ready is not None:
                        pe.wait_ge(ready, before + t + 1)
                    last = nc.tensor.transpose(bank[:, t * P:(t + 1) * P], src(t), ident)
                last.then_inc(done, 1)

            def in_proj(c):
                if c:
                    pe.wait_ge(s["bc_rest_ready"], c)
                turn(w0, lambda t: ln0["hat"][c][:, t, :], s["hat0_T"], s["hat0"], TILES * c)

            def in_proj_x(c):
                pe.wait_ge(s["xn_ready"], c + 1)
                if c:
                    pe.wait_ge(s["sp_relu"], HALVES * c)
                for h, bank in enumerate((w1, w2)):
                    mm(bank[:, :], in_w[:, h, :], xn[c][:, :], start=True, stop=True).then_inc(s["x_mm"], 1)

            def in_proj_z(c, h, bank):
                if c and h:
                    pe.wait_ge(s["conv_tap"], HALVES * (CONV - 1) * (c + 1))
                mm(bank[:, :], in_w[:, HALVES + h, :], xn[c][:, :], start=True, stop=True).then_inc(s["z_mm"], 1)

            def project_dt(c):
                pe.wait_ge(s["u_ready"], HALVES * (c + 1))
                if c:
                    pe.wait_ge(s["z_ready"], HALVES * c + 1)
                for h in range(HALVES):
                    last = mm(w0[0:R, :], xp_dt[:, h, :], u[c][:, h, :], start=(h == 0), stop=(h == HALVES - 1))
                last.then_inc(s["dtr_mm"], 1)

            def dt_proj(c):
                pe.wait_ge(s["dtr_ready"], c + 1)
                if c:
                    pe.wait_ge(s["z_ready"], HALVES * (c + 1))
                for h, bank in enumerate((w1, w2)):
                    mm(bank[:, :], dt_w[:, h, :], dt_r[c][:, :], start=True, stop=True).then_inc(s["dt_mm"], 1)

            def project_bc(c):
                for h in range(HALVES):
                    last = mm(w0[0:PARTS * BCR, :], xp_bc[:, h, :], u[c][:, h, :], start=(h == 0), stop=(h == HALVES - 1))
                last.then_inc(s["bc_mm"], 1)

            def spread_b(i):
                c, n = i // N, i % N
                if n == 0:
                    pe.wait_ge(s["bc_ready"], c + 1)
                if i == 0:
                    pe.wait_ge(s["const_gp"], 1)
                if i >= 1:
                    pe.wait_ge(s["b_copied"], i)
                mm(b_ps[:, :], sel[:, n, :], bc_parts[c][:, :], start=True, stop=True).then_inc(s["b_mm"], 1)

            def spread_c(i):
                c, n = i // N, i % N
                if i >= 2:
                    pe.wait_ge(s["hc_ready"], i - 1)
                mm(c_ps[i % 2][:, :], sel[:, N + n, :], bc_parts[c][:, :], start=True, stop=True).then_inc(s["c_mm"], 1)

            def skip_term(c):
                pe.wait_ge(s["const_gp"], 1 + HALVES)
                if c:
                    pe.wait_ge(s["g_ready"], HALVES * c)
                else:
                    pe.wait_ge(s["z_ready"], HALVES)
                for h in range(HALVES):
                    mm(y_ps[h][:, :], diag_d[:, h, :], u[c][:, h, :], start=True, stop=False)

            def sum_states(i):
                n = i % N
                pe.wait_ge(s["hc_ready"], i + 1)
                for h in range(HALVES):
                    last = mm(y_ps[h][:, :], ident, hc[:, i % RC, h, :], start=False, stop=(n == N - 1))
                last.then_inc(s["y_mm"], 1)

            def out_proj(c):
                pe.wait_ge(s["g_ready"], HALVES * (c + 1))
                if c == 0:
                    pe.wait_ge(s["bc_rest_ready"], CHUNKS)
                    pe.wait_ge(att_in, 16)
                else:
                    pe.wait_ge(s["fm_ready"], c)
                for t in range(TILES):
                    for h in range(HALVES):
                        last = mm(att_banks[c]["proj"][:, t * D:(t + 1) * D], g[c][:, h, t * P:(t + 1) * P], out_w[:, h, :],
                                  start=(h == 0), stop=(h == HALVES - 1))
                last.then_inc(s["proj_mm"], 1)

            def turn_x1(c):
                if c == 0:
                    pe.wait_ge(s["film_biased"], 1)
                else:
                    pe.wait_ge(s["res_ready"], c)
                turn(att_banks[c]["x1T"], lambda t: ln1["hat"][c][:, t, :], s["hat1_T"], s["hat1"], TILES * c)

            def bias_first(c, bank, bias):
                mm(bank[:, :], ones_row, bias.unsqueeze(1).broadcast_to([1, TILES, D]), start=True, stop=False)

            def key_bias(c):
                pe.wait_ge(row_in, 48)
                pe.wait_ge(s["mask_ready"], 2)
                mm(att_banks[c]["k"][:, :], key_lhs[:, :], key_rhs[:, c * CT:(c + 1) * CT], start=True, stop=False)

            def key_proj(c):
                pe.wait_ge(s["x1n_ready"], c + 1)
                mm(att_banks[c]["k"][:, :], att("wk"), x1n[c][:, :], start=False, stop=True).then_inc(s["k_mm"], 1)

            def token_proj(c, bank, weight, done):
                for t in range(TILES):
                    last = mm(bank[:, t * D:(t + 1) * D], x1n[c][:, t * P:(t + 1) * P], att(weight),
                              start=False, stop=(t == TILES - 1))
                last.then_inc(done, 1)

            def query_bias(c):
                if c == 0:
                    pe.wait_ge(s["gated_ready"], 1)
                bias_first(c, att_banks[c]["q"], bq_row)

            def value_bias(c):
                if c:
                    pe.wait_ge(s["b_copied"], CHUNKS * N)
                bias_first(c, att_banks[c]["v"], bv_row)

            def turn_q(c):
                pe.wait_ge(s["q_exp_ready"], c + 1)
                if c:
                    pe.wait_ge(s["y1_ready"], c)
                turn(att_banks[c]["qT"], lambda t: q_exp[c][:, t * P:(t + 1) * P], s["q_T"])

            def turn_k(c):
                pe.wait_ge(s["k_soft_ready"], c + 1)
                turn(att_banks[c]["kT"], lambda t: k_soft[c][:, t * P:(t + 1) * P], s["k_T"])

            def key_values(c, tiles):
                pe.wait_ge(s["v_ready"], TILES * (c + 1))
                pe.wait_ge(s["k_big_ready"], TB * (c + 1))
                if c == 0:
                    pe.wait_ge(s["q_cm_ready"], 1)
                for t in tiles:
                    if t == 3 and c == 0:
                        pe.wait_ge(s["kv_ready"], 1)
                    mm(att_banks[c]["kv"][t][:, :], v_sb[c][:, t, :], k_big[:, t, :, :].rearrange("p j e -> p (j e)"),
                       start=True, stop=True).then_inc(s["kv_mm"], 1)

            def attend(c):
                pe.wait_ge(s["q_cm_ready"], c + 1)
                for t in range(TILES):
                    pe.wait_ge(s["kv_ready"], TILES * c + max(t + 1, 2))
                    for j in range(TB):
                        last = mm(att_banks[c]["y1"][j * S:(j + 1) * S, t * D:(t + 1) * D],
                                  q_cm[c][:, (t * TB + j) * S:(t * TB + j + 1) * S], kv[:, t, j, :],
                                  start=True, stop=True, tile_position=(0, j * S))
                last.then_inc(s["y1_mm"], 1)

            def turn_y(c):
                if c:
                    pe.wait_ge(s["v_ready"], TILES * (c + 1))
                turn(att_banks[c]["yT"], lambda t: ln2["hat"][c][:, t, :], s["hat2_T"], s["hat2"], TILES * c)

            def film_out(c):
                pe.wait_ge(s["fs_ready"], c + 1)
                for t in range(TILES):
                    last = mm(att_banks[c]["out"][:, t * D:(t + 1) * D], fh[c][:, t * P:(t + 1) * P], att("fo_w"), start=True, stop=True)
                last.then_inc(s["fo_mm"], 1)

            def film_factors():
                pe.wait_ge(att_in, 16)
                pe.wait_ge(s["sp_relu"], HALVES * CHUNKS)
                for m in range(2):
                    for k in range(KC):
                        last = mm(w1[:, m * B:(m + 1) * B], film_w[:, k, m * D:(m + 1) * D], cond_s[:, k, :],
                                  start=(k == 0), stop=(k == KC - 1))
                last.then_inc(s["film_mm"], 1)

            def turn_gate():
                pe.wait_ge(s["gate_spread"], 1)
                for c in range(CHUNKS):
                    turn(c_ps[c], lambda t: gate_x[:, c * CT + t * P:c * CT + (t + 1) * P], s["gate_mm"])

            pe.wait_ge(ada_in, 16)
            pe.wait_ge(s["cond_ready"], 1)
            for m in range(3):
                for k in range(KC):
                    last = mm(w1[:, m * B:(m + 1) * B], ada_w[:, k, m * D:(m + 1) * D], cond_s[:, k, :],
                              start=(k == 0), stop=(k == KC - 1))
            last.then_inc(s["ada_mm"], 1)
            pe.wait_ge(ssm_in, 16)
            in_proj(0)
            pe.wait_ge(s["ada_biased"], 1)
            in_proj_x(0)
            in_proj_z(0, 0, y_ps[0])
            in_proj_z(0, 1, y_ps[1])
            turn_gate()
            project_dt(0)
            dt_proj(0)
            project_bc(0)
            for i in range(4):
                spread_b(i)
            spread_c(0)
            for i in range(CHUNKS * N):
                c, n = i // N, i % N
                if c == 0 and n == 0:
                    in_proj(1)
                if c == 0 and n == 2:
                    in_proj_x(1)
                if c == 0 and n == 3:
                    in_proj_z(1, 0, w0)
                if c == 0 and n == 7:
                    in_proj_z(1, 1, w1)
                if c == 0 and n == 8:
                    project_dt(1)
                if c == 0 and n == 9:
                    dt_proj(1)
                    project_bc(1)
                if c == 0 and n == 10:
                    film_factors()
                if c == 1 and n == 1:
                    out_proj(0)
                if c == 1 and n == 4:
                    turn_x1(0)
                if c == 1 and n == 5:
                    key_bias(0)
                    key_proj(0)
                if c == 1 and n == 6:
                    query_bias(0)
                    token_proj(0, w0, "wq", s["q_mm"])
                if c == 1 and n == 7:
                    value_bias(0)
                    token_proj(0, w1, "wv", s["v_mm"])
                if c == 1 and n == 9:
                    turn_q(0)
                    turn_k(0)
                if c == 1 and n == 10:
                    key_values(0, (0, 1))
                if c == 1 and n == 11:
                    key_values(0, (2,))
                if c == 1 and n == 12:
                    key_values(0, (3,))
                if c == 1 and n == 13:
                    attend(0)
                if c == 1 and n == 15:
                    turn_y(0)
                if i + 1 < CHUNKS * N:
                    spread_c(i + 1)
                if n == 0:
                    if c:
                        sum_states(i - 1)
                    skip_term(c)
                else:
                    sum_states(i - 1)
                if i + 4 < CHUNKS * N:
                    spread_b(i + 4)
            sum_states(CHUNKS * N - 1)
            film_out(0)
            out_proj(1)
            key_bias(1)
            query_bias(1)
            value_bias(1)
            turn_x1(1)
            key_proj(1)
            token_proj(1, c_ps[1], "wq", s["q_mm"])
            token_proj(1, b_ps, "wv", s["v_mm"])
            turn_k(1)
            turn_q(1)
            key_values(1, range(TILES))
            attend(1)
            turn_y(1)
            film_out(1)


def kernel(**inputs):
    import numpy as np
    import concourse.bacc as bacc
    from concourse.bass_utils import run_bass_kernel_spmd

    w = {name: np.ascontiguousarray(a) for name, a in inputs.items()}

    def slices(a):
        return np.ascontiguousarray(a.reshape(-1, P, a.shape[-1]).transpose(1, 0, 2)).reshape(P, -1)

    def column(a):
        return slices(a.reshape(-1, 1))

    def high(a):
        return np.concatenate([a, np.zeros((P - a.shape[0], a.shape[1]), a.dtype)])

    eye = np.eye(P, dtype=np.float32)
    xp = w["L0_cond_x_proj_w"].T
    parts = {
        "cond": slices(w["cond_2048"].T), "ada_w": slices(w["L0_cond_ada_w"].T), "ada_b": column(w["L0_cond_ada_b"]),
        "ln_g": column(w["L0_cond_ln_g"]), "ln_b": column(w["L0_cond_ln_b"]),
        "ident": eye, "in_w": w["L0_cond_in_proj_w"].T, "conv_w": slices(w["L0_cond_conv_w"]),
        "conv_b": column(w["L0_cond_conv_b"]), "xp_dt": slices(xp[:, :R]),
        "xp_bc": slices(np.concatenate([xp[:, R:]] * PARTS, axis=1)), "dt_w": high(w["L0_cond_dt_proj_w"].T),
        "dt_b": column(w["L0_cond_dt_proj_b"]), "a_log": slices(w["L0_cond_A_log"]),
        "d_skip": column(w["L0_cond_D_param"]),
        "sel_seed": high(np.concatenate([np.eye(BCR, dtype=np.float32)] * PARTS)),
        "out_w": slices(w["L0_cond_out_proj_w"].T), "norm_s": column(w["L1_cond_norm_scale"]),
        "norm_b": column(w["L1_cond_norm_bias"]), "wq": w["L1_cond_Wq"], "wk": w["L1_cond_Wk"], "wv": w["L1_cond_Wv"],
        "film_w": slices(w["L1_cond_film_emb_W"]), "film_b": column(w["L1_cond_film_emb_b"]),
        "fnorm_s": column(w["L1_cond_film_norm_scale"]), "fnorm_b": column(w["L1_cond_film_norm_bias"]),
        "fo_w": w["L1_cond_film_out_W"],
        "heads": np.kron(np.eye(D // HEAD, dtype=np.float32), np.ones((HEAD, HEAD), np.float32)),
    }

    def pack(names):
        return np.ascontiguousarray(np.concatenate([parts[name] for name, _ in names], axis=1))

    ones = np.ones((1, D), np.float32)
    mask = w["mask_BxS_ik0"]
    feeds = {
        "x": w["x"].reshape(B * S, D), "pack_ada": pack(PACK_ADA), "pack_ssm": pack(PACK_SSM), "pack_att": pack(PACK_ATT),
        "rows": np.concatenate([w["L1_cond_bq"][None], w["L1_cond_bv"][None], ones], axis=1),
        "key_rows": np.concatenate([ones, w["L1_cond_bk"][None]]),
        "mask_row": mask.reshape(1, B * S), "mask_tok": np.ascontiguousarray(mask.reshape(-1, P).T),
        "film_ob": w["L1_cond_film_out_b"],
    }
    nc = bacc.Bacc("TRN2", target_bir_lowering=False, num_devices=1)
    args = [nc.dram_tensor(f"in_{n}_dram", a.shape, mybir.dt.from_np(a.dtype), kind="ExternalInput").ap()
            for n, a in feeds.items()]
    out = nc.dram_tensor("out_0_dram", (B * S, D), mybir.dt.float32, kind="ExternalOutput").ap()
    mamba_attention_kernel(nc, *args, out)
    r = run_bass_kernel_spmd(nc, [{f"in_{n}_dram": a for n, a in feeds.items()}], core_ids=[0])
    return r.results[0]["out_0_dram"].reshape(B, S, D)
```

```python
import concourse.bass as bass
from concourse import mybir
from contextlib import ExitStack

B, S, D = 32, 32, 128
DI, N, R, CONV = 256, 16, 64, 4
HEAD = 8
E = 256
EPS = 1e-5
P = 128
HALVES = DI // P
CHUNKS = 2
CB_ = B // CHUNKS
CT = CB_ * S
TILES = CT // P
TB = P // S
KC = E // P
PARTS = 3
BCR = 2 * N
MASKED = -1e30

PACK_ADA = [("cond", KC * B), ("ada_w", KC * 3 * D), ("ada_b", 3), ("ln_g", 1), ("ln_b", 1)]
PACK_SSM = [("ident", P), ("in_w", 2 * DI), ("conv_w", HALVES * CONV), ("conv_b", HALVES), ("xp_dt", HALVES * R),
            ("xp_bc", HALVES * PARTS * BCR), ("dt_w", DI), ("dt_b", HALVES), ("a_log", HALVES * N),
            ("d_skip", HALVES), ("sel_seed", BCR)]
PACK_ATT = [("out_w", HALVES * D), ("norm_s", 1), ("norm_b", 1), ("wq", D), ("wk", D), ("wv", D),
            ("film_w", KC * 2 * D), ("film_b", 2), ("fnorm_s", 1), ("fnorm_b", 1), ("fo_w", D), ("heads", D)]


def columns(pack):
    at, out = 0, {}
    for name, width in pack:
        out[name] = (at, at + width)
        at += width
    return out, at


def mamba_attention_kernel(nc, x, pack_ada, pack_ssm, pack_att, rows, key_rows, mask_row, mask_tok, film_ob, out):
    fp32, bf16, i32 = mybir.dt.float32, mybir.dt.bfloat16, mybir.dt.int32
    ALU, ACT, AX = mybir.AluOpType, mybir.ActivationFunctionType, mybir.AxisListType

    with ExitStack() as ctx:
        def sb(name, shape, dt=fp32):
            return ctx.enter_context(nc.sbuf_tensor(name, shape, dt))

        def pb(name, shape):
            return ctx.enter_context(nc.psum_tensor(name, shape, fp32))

        def sem(name):
            return ctx.enter_context(nc.semaphore(name))

        x_sb = sb("x_sb", [P, CHUNKS * TILES, D])
        at_ada, n_ada = columns(PACK_ADA)
        at_ssm, n_ssm = columns(PACK_SSM)
        at_att, n_att = columns(PACK_ATT)
        ada_sb = sb("ada_sb", [P, n_ada])
        ssm_sb = sb("ssm_sb", [P, n_ssm])
        att_sb = sb("att_sb", [P, n_att])
        rows_sb = sb("rows_sb", [1, 3 * D])
        key_lhs = sb("key_lhs", [2, D])
        key_rhs = sb("key_rhs", [2, B * S])
        mask_row_i = sb("mask_row_i", [1, B * S], i32)
        mask_tok_i = sb("mask_tok_i", [P, CHUNKS * TILES], i32)
        film_ob_bc = sb("film_ob_bc", [P, D])

        def ada(name):
            return ada_sb[:, at_ada[name][0]:at_ada[name][1]]

        def ssm(name):
            return ssm_sb[:, at_ssm[name][0]:at_ssm[name][1]]

        def att(name):
            return att_sb[:, at_att[name][0]:at_att[name][1]]

        cond_in = ada("cond")
        ada_w = ada("ada_w").rearrange("p (k e) -> p k e", k=KC)
        ident = ssm("ident")
        in_w = ssm("in_w").rearrange("p (m e) -> p m e", e=P)
        conv_w = ssm("conv_w").rearrange("p (h k) -> p h k", h=HALVES)
        conv_b = ssm("conv_b")
        xp_dt = ssm("xp_dt").rearrange("p (h r) -> p h r", h=HALVES)
        xp_bc = ssm("xp_bc").rearrange("p (h r) -> p h r", h=HALVES)
        dt_w = ssm("dt_w")[0:R, :].rearrange("r (h d) -> r h d", h=HALVES)
        dt_b = ssm("dt_b")
        a_log = ssm("a_log")
        d_skip = ssm("d_skip")
        sel_seed = ssm("sel_seed")[0:PARTS * BCR, :]
        out_w = att("out_w").rearrange("p (h e) -> p h e", h=HALVES)
        film_w = att("film_w").rearrange("p (k e) -> p k e", k=KC)
        heads = att("heads")
        bq_row, bv_row, ones_row = (rows_sb[0:1, i * D:(i + 1) * D] for i in range(3))

        cond_s = sb("cond_s", [P, KC, B])
        adas = sb("adas", [P, 3, B])
        ln_tmp = sb("ln_tmp", [P, B])
        ln_mul = sb("ln_mul", [P, B])
        ln_add = sb("ln_add", [P, B])
        films = sb("films", [P, 2, B])
        film_tmp = sb("film_tmp", [P, B])
        film_mul = sb("film_mul", [P, B])
        film_add = sb("film_add", [P, B])
        gate_tok = sb("gate_tok", [P, CHUNKS * TILES, D])
        a_exp = sb("a_exp", [P, HALVES * N])
        a_neg = sb("a_neg", [P, HALVES * N])
        sel = sb("sel", [PARTS * BCR, BCR, P], bf16)
        diag_d = sb("diag_d", [P, HALVES, P])
        valid = sb("valid", [P, CHUNKS * TILES])
        half_neg = sb("half_neg", [P, TILES])

        def per_chunk(name, shape, dt=fp32):
            return [sb(f"{name}{c}", shape, dt) for c in range(CHUNKS)]

        def shared(name, shape, dt=fp32):
            return [sb(name, shape, dt)] * CHUNKS

        def norm_buffers(name):
            return {"stats": shared(name + "_stats", [P, TILES, 6]), "mv": shared(name + "_mv", [P, TILES, 2]),
                    "var": shared(name + "_var", [P, TILES]), "rstd": shared(name + "_rstd", [P, TILES]),
                    "hat": shared(name + "_hat", [P, TILES, D])}

        ln0, ln1, ln2 = norm_buffers("ln0"), norm_buffers("ln1"), norm_buffers("ln2")
        xn = shared("xn", [P, CT])
        u = per_chunk("u", [P, HALVES, CT])
        z_s = per_chunk("z_s", [P, HALVES, CT])
        bc_parts = per_chunk("bc_parts", [PARTS * BCR, CT], bf16)
        bc_rest = shared("bc_rest", [PARTS * BCR, CT])
        dt_r = shared("dt_r", [R, CT])
        sp = shared("sp", [P, HALVES, CT])
        dt = per_chunk("dt", [P, HALVES, CT])
        dtu = per_chunk("dtu", [P, HALVES, CT])
        g = shared("g", [P, HALVES, CT])
        x1 = shared("x1", [P, TILES, D])
        x1b = shared("x1b", [P, TILES, D])
        x1n = shared("x1n", [P, CT])
        k_max = shared("k_max", [P, CB_])
        k_exp = shared("k_exp", [P, CT])
        k_sum = shared("k_sum", [P, CB_])
        k_den = shared("k_den", [P, CB_])
        k_inv = shared("k_inv", [P, CB_])
        k_soft = shared("k_soft", [P, CT])
        q_max = shared("q_max", [P, TILES * D // HEAD])
        q_exp = shared("q_exp", [P, TILES * D])
        q_sum = shared("q_sum", [P, TILES * D // HEAD])
        q_inv = shared("q_inv", [P, TILES * D // HEAD])
        v_sb = shared("v_sb", [P, TILES, D])
        q_cm = shared("q_cm", [P, CT])
        k_big = sb("k_big", [P, TILES, TB, D])
        kv = sb("kv", [P, TILES, TB, D])
        gate_x = kv[:, 0:2, :, :].rearrange("p t j e -> p (t j e)")
        y1 = shared("y1", [P, TILES, D])
        fh = [xn[0], sb("fh1", [P, CT])]
        res = per_chunk("res", [P, TILES, D])

        RD, RB, RH, RC = 4, 5, 3, 3
        EARLY = 1
        LEAD = 2
        SIDE, SIDE_AT = 5, 2
        c_bc = sb("c_bc", [P, CT])
        decay = sb("decay", [P, RD, HALVES, CT])
        b_bc = sb("b_bc", [P, RB, CT])
        drive = sb("drive", [P, RD, HALVES, CT])
        state = sb("state", [P, RH, HALVES, CT])
        hc = sb("hc", [P, RC, HALVES, CT])

        warm_in = sb("warm_in", [P, P])

        y_ps = [pb(f"y_ps{h}", [P, CT]) for h in range(HALVES)]
        c_ps = [pb(f"c_ps{i}", [P, CT]) for i in range(2)]
        b_ps = pb("b_ps", [P, CT])
        w0, w1, w2 = (pb(f"w{i}", [P, CT]) for i in range(3))

        att_banks = [
            {"proj": w0, "x1T": (w1,), "k": w2, "q": w0, "v": w1, "qT": w0, "kT": w2, "kv": (w1, w2, w0, w1), "y1": w2,
             "yT": (w0,), "out": (y_ps[0],)},
            {"proj": w2, "x1T": (w1, y_ps[0]), "k": c_ps[0], "q": c_ps[1], "v": b_ps, "qT": w2, "kT": y_ps[0],
             "kv": (y_ps[1], w0, w1, c_ps[0]), "y1": c_ps[1], "yT": (b_ps, w1), "out": (w2, c_ps[0])},
        ]

        bc_banks = [c_ps[0], w0]

        tile_parts = [[(0, 1, 2, 3)], [(0, 1), (2, 3)]]

        def parts_of(c):
            for p, tiles in enumerate(tile_parts[c]):
                a, b = tiles[0], tiles[-1] + 1
                yield len(tile_parts[0]) * c + p + 1, p, tiles, slice(a * P, b * P), slice(a * TB, b * TB)

        x_in = [sem(f"x_in{c}") for c in range(CHUNKS)]
        ada_in, ssm_in, att_in, row_in, mask_in, out_done = (
            sem(n) for n in ("ada_in", "ssm_in", "att_in", "row_in", "mask_in", "out_done"))
        names = """cleared const_gp cond_ready ada_mm ada_biased ln_tmp_ready ln_affine gate_spread gate_mm gate_ready mask_neg film_mm
            film_biased film_affine a_exp_ready a_ready mask_ready
            stat0 aggr0 var0 rstd0 hat0 hat0_T xg_ready xn_ready x_mm z_mm conv_first conv_tap u_ready z_ready
            bc_mm bc_top bc_rest_ready bc_mid bc_ready dtr_mm dtr_ready dt_mm sp_abs sp_relu sp_exp_ready sp_ready dt_ready
            dtu_ready b_mm b_copied drive_ready drive_early c_copied hc_side decay_ready scan_done c_mm hc_ready y_mm
            g_ready proj_mm gated_ready x1_ready x1b_ready stat1 aggr1 var1 rstd1 hat1 hat1_T x1n_ready
            k_mm k_max_ready k_sub_ready k_exp_ready k_sum_ready k_den_ready k_inv_ready k_soft_ready
            q_mm q_max_ready q_sub_ready q_exp_ready q_sum_ready q_inv_ready v_mm v_ready
            q_T q_cm_ready k_T k_big_ready kv_mm kv_ready y1_mm y1_ready
            stat2 aggr2 var2 rstd2 hat2 hat2_T fm_ready fh_ready fs_ready fo_mm res_ready""".split()
        s = {name: sem(name) for name in names}

        def batches(ap):
            return ap.rearrange("p (b t) -> p b t", t=S)

        def over_steps(ap):
            return ap.unsqueeze(2).broadcast_to([P, CB_, S])

        def over_head(ap):
            return ap.unsqueeze(2).broadcast_to([P, TILES * D // HEAD, HEAD])

        def in_heads(ap):
            return ap.rearrange("p (g e) -> p g e", e=HEAD)

        def mine(c):
            return slice(c * CB_, (c + 1) * CB_)

        def tiled(ap):
            return ap.rearrange("p (t e) -> p t e", e=D)

        def drives(i):
            return i if i > EARLY else i + 1

        def shared_step(i):
            return i % SIDE == SIDE_AT

        def sides(i):
            return (i - SIDE_AT) // SIDE + 1

        block = ctx.enter_context(nc.Block())

        @block.sync
        def _(sync):
            x_v = x.rearrange("(n p) d -> p n d", p=P)
            sync.dma_start(x_sb[:, 0:TILES, :], x_v[:, 0:TILES, :]).then_inc(x_in[0], 16)
            sync.dma_start(ssm_sb[:, :], pack_ssm).then_inc(ssm_in, 16)
            sync.dma_start(x_sb[:, TILES:, :], x_v[:, TILES:, :]).then_inc(x_in[1], 16)
            sync.dma_start(mask_row_i[:, :], mask_row).then_inc(mask_in, 16)
            sync.dma_start(mask_tok_i[:, :], mask_tok).then_inc(mask_in, 16)
            out_v = out.rearrange("(n p) d -> p n d", p=P)
            for c in range(CHUNKS):
                for count, _, tiles, _, _ in parts_of(c):
                    sync.wait_ge(s["res_ready"], count)
                    a, b = tiles[0], tiles[-1] + 1
                    sync.dma_start(out_v[:, c * TILES + a:c * TILES + b, :], res[c][:, a:b, :]).then_inc(out_done, 16)
            sync.wait_ge(out_done, 16 * sum(len(p) for p in tile_parts))

        @block.gpsimd
        def _(gp):
            tt, ts = nc.gpsimd.tensor_tensor, nc.gpsimd.tensor_scalar

            def rstd(k, buf, c):
                gp.wait_ge(s[f"var{k}"], c + 1)
                if k == 0 and c == 0:
                    gp.wait_ge(s["cleared"], 5)
                tt(buf["rstd"][c][:, :], buf["var"][c][:, :], half_neg[:, :], ALU.pow).then_inc(s[f"rstd{k}"], 1)

            def drive_step(i):
                c = i // N
                gp.wait_ge(s["b_copied"], i + 1)
                if i >= RD:
                    gp.wait_ge(s["scan_done"], i - RD + 1)
                if i == 0:
                    for h in range(HALVES):
                        gp.wait_ge(s["dtu_ready"], h + 1)
                        last = tt(drive[:, 0, h, :], dtu[0][:, h, :], b_bc[:, 0, :], ALU.mult)
                    last.then_inc(s["drive_ready"], 1)
                    return
                if i % N == 0:
                    gp.wait_ge(s["dtu_ready"], HALVES * (c + 1))
                tt(drive[:, i % RD, :, :], dtu[c][:, :, :],
                   b_bc[:, i % RB, :].unsqueeze(1).broadcast_to([P, HALVES, CT]), ALU.mult).then_inc(s["drive_ready"], 1)

            def weigh_side(i):
                gp.wait_ge(s["c_copied"], sides(i))
                gp.wait_ge(s["scan_done"], i + 1)
                if i >= RC:
                    gp.wait_ge(s["y_mm"], i - RC + 1)
                tt(hc[:, i % RC, 1, :], state[:, i % RH, 1, :], c_bc[:, :], ALU.mult).then_inc(s["hc_side"], 1)

            nc.gpsimd.memset(warm_in[:, :], 0.0).then_inc(s["cleared"], 1)
            nc.gpsimd.memset(half_neg[:, :], -0.5).then_inc(s["cleared"], 1)
            nc.gpsimd.memset(decay[:, :, :, :].rearrange("p r h (b t) -> p (r h b) t", t=S)[:, :, 0:1], 0.0)\
                .then_inc(s["cleared"], 1)
            nc.gpsimd.memset(key_rhs[:, :], 1.0).then_inc(s["cleared"], 1)
            nc.gpsimd.memset(k_big[:, :, :, :], 0.0).then_inc(s["cleared"], 1)
            rstd(0, ln0, 0)
            gp.wait_ge(ssm_in, 16)
            ts(sel[:, :, :], sel_seed.unsqueeze(2).broadcast_to([PARTS * BCR, BCR, P]), 1.0, 0.0, ALU.mult, ALU.add)\
                .then_inc(s["const_gp"], 1)
            for h in range(HALVES):
                ts(diag_d[:, h, :], ident, d_skip[:, h:h + 1], 0.0, ALU.mult, ALU.add).then_inc(s["const_gp"], 1)

            def add_x(c):
                gp.wait_ge(s["gated_ready"], c + 1)
                tt(x1[c][:, :, :], x1[c][:, :, :], x_sb[:, c * TILES:(c + 1) * TILES, :], ALU.add)\
                    .then_inc(s["x1_ready"], 1)

            def steps_dtu(c, h):
                gp.wait_ge(s["u_ready"], HALVES * (c + 1))
                gp.wait_ge(s["dt_ready"], HALVES * c + h + 1)
                tt(dtu[c][:, h, :], dt[c][:, h, :], u[c][:, h, :], ALU.mult).then_inc(s["dtu_ready"], 1)

            def late_sums(c):
                gp.wait_ge(s["x1_ready"], c + 1)
                gp.wait_ge(row_in, 48)
                tt(x1b[c][:, :, :], x1[c][:, :, :], film_ob_bc[:, :].unsqueeze(1).broadcast_to([P, TILES, D]),
                   ALU.add).then_inc(s["x1b_ready"], 1)

            def adaptive_shift(c):
                gp.wait_ge(s["xg_ready"], c + 1)
                gp.wait_ge(s["ln_affine"], 2)
                tt(batches(xn[c][:, :]), batches(xn[c][:, :]), over_steps(ln_add[:, mine(c)]), ALU.add)\
                    .then_inc(s["xn_ready"], 1)

            def film_shift(c):
                gp.wait_ge(s["fm_ready"], c + 1)
                gp.wait_ge(s["film_affine"], 3)
                tt(batches(fh[c][:, :]), batches(fh[c][:, :]), over_steps(film_add[:, mine(c)]), ALU.add)\
                    .then_inc(s["fh_ready"], 1)

            def soft_keys(c):
                gp.wait_ge(s["k_inv_ready"], c + 1)
                tt(batches(k_soft[c][:, :]), batches(k_exp[c][:, :]), over_steps(k_inv[c][:, :]), ALU.mult)\
                    .then_inc(s["k_soft_ready"], 1)

            gp.wait_ge(s["ada_biased"], 1)
            ts(gate_x.rearrange("p (b t) -> p b t", t=S), adas[:, 2, :].unsqueeze(2).broadcast_to([P, B, S]), 1.0, 0.0,
               ALU.mult, ALU.add).then_inc(s["gate_spread"], 1)
            gp.dma_start(rows_sb[:, :], rows).then_inc(row_in, 16)
            gp.dma_start(key_lhs[:, :], key_rows).then_inc(row_in, 16)
            gp.dma_start(film_ob_bc[:, :], film_ob.partition_broadcast(P)).then_inc(row_in, 16)
            rstd(0, ln0, 1)
            gp.wait_ge(mask_in, 32)
            ts(key_rhs[0:1, :], mask_row_i[:, :], 1.0, MASKED, ALU.is_equal, ALU.mult).then_inc(s["mask_ready"], 1)
            ts(valid[:, :], mask_tok_i[:, :], 1.0, -1.0, ALU.is_equal, ALU.mult).then_inc(s["mask_neg"], 1)
            gp.wait_ge(s["mask_neg"], 1)
            ts(valid[:, :], valid[:, :], 1.0, 1.0, ALU.mult, ALU.add).then_inc(s["mask_ready"], 1)
            drive_step(0)
            for i in range(CHUNKS * N):
                c, n = i // N, i % N
                if i + LEAD < CHUNKS * N:
                    drive_step(i + LEAD)
                if i > 0 and shared_step(i - 1):
                    weigh_side(i - 1)
                if c == 0 and n == 0:
                    adaptive_shift(1)
                if c == 1 and n == 3:
                    add_x(0)
                if c == 0 and n == 13:
                    steps_dtu(1, 0)
                if c == 1 and n == 4:
                    rstd(1, ln1, 0)
                if c == 1 and n == 9:
                    soft_keys(0)
                if c == 1 and n == 10:
                    late_sums(0)
                if c == 1 and n == 14:
                    rstd(2, ln2, 0)
            rstd(1, ln1, 1)
            film_shift(0)
            rstd(2, ln2, 1)
            gp.wait_ge(s["res_ready"], 1)
            late_sums(1)

        @block.scalar
        def _(act):
            A = nc.scalar.activation
            act.dma_start(ada_sb[:, :], pack_ada).then_inc(ada_in, 16)
            act.dma_start(att_sb[:, :], pack_att).then_inc(att_in, 16)

            act.wait_ge(ada_in, 16)
            A(cond_s[:, :, :].rearrange("p k b -> p (k b)"), cond_in, ACT.Silu).then_inc(s["cond_ready"], 1)

            def conv_start(c):
                for h, bank in enumerate((w1, w2)):
                    act.wait_ge(s["x_mm"], HALVES * c + h + 1)
                    A(u[c][:, h, :], bank[:, :], ACT.Identity, bias=conv_b[:, h:h + 1],
                      scale=conv_w[:, h, CONV - 1:CONV]).then_inc(s["conv_first"], 1)

            def silu_u(c):
                for h in range(HALVES):
                    act.wait_ge(s["conv_tap"], HALVES * (CONV - 1) * c + HALVES * (CONV - 2) + h + 1)
                    A(u[c][:, h, :], u[c][:, h, :], ACT.Silu).then_inc(s["u_ready"], 1)

            def silu_z(c, banks):
                for h, bank in enumerate(banks):
                    act.wait_ge(s["z_mm"], HALVES * c + h + 1)
                    A(z_s[c][:, h, :], bank[:, :], ACT.Silu).then_inc(s["z_ready"], 1)

            def copy_dt_rows(c):
                act.wait_ge(s["dtr_mm"], c + 1)
                A(dt_r[c][:, :], w0[0:R, :], ACT.Copy).then_inc(s["dtr_ready"], 1)

            def top_bc(c):
                act.wait_ge(s["bc_mm"], c + 1)
                A(bc_parts[c][:, :], bc_banks[c][0:PARTS * BCR, :], ACT.Copy).then_inc(s["bc_top"], 1)

            def copy_gates():
                for c in range(CHUNKS):
                    act.wait_ge(s["gate_mm"], c + 1)
                    A(gate_tok[:, c * TILES:(c + 1) * TILES, :], tiled(c_ps[c][:, :]), ACT.Copy)\
                        .then_inc(s["gate_ready"], 1)

            def softplus(c, halves=range(HALVES)):
                for h in halves:
                    bank = (w1, w2)[h]
                    act.wait_ge(s["dt_mm"], HALVES * c + h + 1)
                    A(sp[c][:, h, :], bank[:, :], ACT.Abs, bias=dt_b[:, h:h + 1]).then_inc(s["sp_abs"], 1)
                    if c:
                        A(dt[c][:, h, :], bank[:, :], ACT.Relu, bias=dt_b[:, h:h + 1]).then_inc(s["sp_relu"], 1)

            def softplus_end(c):
                act.wait_ge(s["sp_abs"], HALVES * (c + 1))
                for h in range(HALVES):
                    A(sp[c][:, h, :], sp[c][:, h, :], ACT.Exp, scale=-1.0).then_inc(s["sp_exp_ready"], 1)
                for h in range(HALVES):
                    act.wait_ge(s["sp_exp_ready"], HALVES * c + h + 1)
                    A(sp[c][:, h, :], sp[c][:, h, :], ACT.Ln, bias=1.0).then_inc(s["sp_ready"], 1)

            def decays(i):
                c, n = i // N, i % N
                if n == 0:
                    act.wait_ge(s["dt_ready"], HALVES * (c + 1))
                    act.wait_ge(s["a_ready"], 1)
                    act.wait_ge(s["cleared"], 3)
                if i >= RD:
                    act.wait_ge(s["scan_done"], i - RD + 1)
                for h in range(HALVES):
                    A(batches(decay[:, i % RD, h, :])[:, :, 1:S], batches(dt[c][:, h, :])[:, :, 1:S], ACT.Exp,
                      scale=a_neg[:, h * N + n:h * N + n + 1]).then_inc(s["decay_ready"], 1)

            def copy_b(i):
                act.wait_ge(s["b_mm"], i + 1)
                if i - RB == EARLY:
                    act.wait_ge(s["drive_early"], 1)
                elif i >= RB:
                    act.wait_ge(s["drive_ready"], drives(i - RB))
                A(b_bc[:, i % RB, :], b_ps[:, :], ACT.Copy).then_inc(s["b_copied"], 1)

            def copy_c(i):
                act.wait_ge(s["c_mm"], i + 1)
                if i >= SIDE:
                    act.wait_ge(s["hc_ready"], i - SIDE + 1)
                    act.wait_ge(s["hc_side"], sides(i) - 1)
                A(c_bc[:, :], c_ps[i % 2][:, :], ACT.Copy).then_inc(s["c_copied"], 1)

            def x1_affine(c):
                if c == 0:
                    act.wait_ge(att_in, 16)
                for count, p, _, tokens, _ in parts_of(c):
                    act.wait_ge(s["hat1_T"], count)
                    A(x1n[c][:, tokens], att_banks[c]["x1T"][p][:, tokens], ACT.Identity, bias=att("norm_b"),
                      scale=att("norm_s")).then_inc(s["x1n_ready"], 1)

            def values(c):
                act.wait_ge(s["v_mm"], c + 1)
                for t in range(TILES):
                    A(v_sb[c][:, t, :], tiled(att_banks[c]["v"][:, :])[:, t, :], ACT.Copy, scale=valid[:, c * TILES + t:c * TILES + t + 1])\
                        .then_inc(s["v_ready"], 1)

            def key_exp(c):
                act.wait_ge(s["k_sub_ready"], c + 1)
                A(k_exp[c][:, :], k_exp[c][:, :], ACT.Exp).then_inc(s["k_exp_ready"], 1)

            def query_exp(c):
                act.wait_ge(s["q_sub_ready"], c + 1)
                A(q_exp[c][:, :], q_exp[c][:, :], ACT.Exp).then_inc(s["q_exp_ready"], 1)

            def copy_q(c):
                act.wait_ge(s["q_T"], c + 1)
                A(q_cm[c][:, :], att_banks[c]["qT"][:, :], ACT.Copy).then_inc(s["q_cm_ready"], 1)

            def turned(c):
                if c == 0:
                    copy_q(c)
                act.wait_ge(s["k_T"], c + 1)
                act.wait_ge(s["cleared"], 5)
                if c:
                    act.wait_ge(s["kv_mm"], TILES * c)
                for j in range(TB if c == 0 else TB // 2):
                    A(k_big[j * S:(j + 1) * S, :, j, :], tiled(att_banks[c]["kT"][j * S:(j + 1) * S, :]), ACT.Copy)\
                        .then_inc(s["k_big_ready"], 1)

            def film_silu(c):
                for count, _, _, tokens, _ in parts_of(c):
                    act.wait_ge(s["fh_ready"], count)
                    A(fh[c][:, tokens], fh[c][:, tokens], ACT.Silu).then_inc(s["fs_ready"], 1)

            conv_start(0)
            silu_z(0, y_ps)
            copy_gates()
            silu_u(0)
            copy_dt_rows(0)
            nc.scalar.preload_act_table_set("natural_log_exp_and_others")
            A(a_exp[:, :], a_log, ACT.Exp).then_inc(s["a_exp_ready"], 1)
            softplus(0)
            top_bc(0)
            softplus_end(0)
            copy_b(0)
            copy_b(1)
            decays(0)
            copy_b(2)
            decays(1)
            copy_b(3)
            decays(2)
            for i in range(CHUNKS * N):
                c, n = i // N, i % N
                if shared_step(i):
                    copy_c(i)
                if i + LEAD + 1 < CHUNKS * N:
                    decays(i + LEAD + 1)
                if i + LEAD + 2 < CHUNKS * N:
                    copy_b(i + LEAD + 2)
                if c == 0 and n == 1:
                    conv_start(1)
                if c == 0 and n == 6:
                    silu_u(1)
                    silu_z(1, (w0, w1))
                    nc.scalar.preload_act_table_set("natural_log_exp_and_others")
                if c == 0 and n == 7:
                    copy_dt_rows(1)
                if c == 0 and n == 8:
                    softplus(1, (0,))
                if c == 0 and n == 9:
                    softplus(1, (1,))
                    top_bc(1)
                if c == 0 and n == 10:
                    softplus_end(1)
                if c == 1 and n == 5:
                    x1_affine(0)
                if c == 1 and n == 8:
                    key_exp(0)
                if c == 1 and n == 9:
                    query_exp(0)
                    values(0)
                if c == 1 and n == 10:
                    turned(0)
            x1_affine(1)
            key_exp(1)
            values(1)
            turned(1)
            query_exp(1)
            copy_q(1)
            film_silu(0)
            film_silu(1)

        @block.vector
        def _(dve):
            V = nc.vector

            def norm_stats(k, buf, c, src):
                if k:
                    dve.wait_ge(s[("", "x1_ready", "y1_ready")[k]], c + 1)
                for t in range(TILES):
                    V.bn_stats(buf["stats"][c][:, t, :], src(t)).then_inc(s[f"stat{k}"], 1)
                dve.wait_ge(s[f"stat{k}"], TILES * (c + 1))
                for t in range(TILES):
                    V.bn_aggr(buf["mv"][c][:, t, :], buf["stats"][c][:, t, :]).then_inc(s[f"aggr{k}"], 1)
                dve.wait_ge(s[f"aggr{k}"], TILES * (c + 1))
                V.tensor_scalar(buf["var"][c][:, :], buf["mv"][c][:, :, 1:2].rearrange("p t o -> p (t o)"), EPS, None,
                                ALU.add).then_inc(s[f"var{k}"], 1)

            def normalise(k, buf, c, src):
                dve.wait_ge(s[f"rstd{k}"], c + 1)
                for t in range(TILES):
                    V.tensor_scalar(buf["hat"][c][:, t, :], src(t), buf["mv"][c][:, t, 0:1], buf["rstd"][c][:, t:t + 1],
                                    ALU.subtract, ALU.mult).then_inc(s[f"hat{k}"], 1)

            def x_tile(c):
                return lambda t: x_sb[:, c * TILES + t, :]

            def adaptive(c):
                dve.wait_ge(s["hat0_T"], c + 1)
                V.tensor_tensor(batches(xn[c][:, :]), batches(w0[:, :]), over_steps(ln_mul[:, mine(c)]), ALU.mult)\
                    .then_inc(s["xg_ready"], 1)
                if c == 0:
                    dve.wait_ge(s["xg_ready"], c + 1)
                    V.tensor_tensor(batches(xn[c][:, :]), batches(xn[c][:, :]), over_steps(ln_add[:, mine(c)]), ALU.add)\
                        .then_inc(s["xn_ready"], 1)

            def conv_taps(c, backs=range(1, CONV)):
                for back in backs:
                    for h, bank in enumerate((w1, w2)):
                        if back == 1:
                            dve.wait_ge(s["conv_first"], HALVES * c + h + 1)
                        else:
                            dve.wait_ge(s["conv_tap"], HALVES * ((CONV - 1) * c + back - 2) + h + 1)
                        V.scalar_tensor_tensor(
                            out=batches(u[c][:, h, :])[:, :, back:S], in0=batches(bank[:, :])[:, :, 0:S - back],
                            scalar=conv_w[:, h, CONV - 1 - back:CONV - back],
                            in1=batches(u[c][:, h, :])[:, :, back:S], op0=ALU.mult, op1=ALU.add)\
                            .then_inc(s["conv_tap"], 1)

            def rest_bc(c):
                dve.wait_ge(s["bc_top"], c + 1)
                V.tensor_tensor(bc_rest[c][:, :], bc_banks[c][0:PARTS * BCR, :], bc_parts[c][:, :], ALU.subtract)\
                    .then_inc(s["bc_rest_ready"], 1)

            def split_bc(c):
                dve.wait_ge(s["bc_rest_ready"], c + 1)
                for part in range(1, PARTS):
                    r = slice(part * BCR, (part + 1) * BCR)
                    V.tensor_copy(bc_parts[c][r, :], bc_rest[c][r, :]).then_inc(s["bc_mid"], 1)
                dve.wait_ge(s["bc_mid"], 2 * (c + 1))
                V.tensor_tensor(bc_parts[c][r, :], bc_rest[c][r, :], bc_parts[c][r, :], ALU.subtract)\
                    .then_inc(s["bc_ready"], 1)

            def relu_dt(c):
                for h, bank in enumerate((w1, w2)):
                    dve.wait_ge(s["sp_abs"], HALVES * c + h + 1)
                    V.tensor_scalar(dt[c][:, h, :], bank[:, :], dt_b[:, h:h + 1], 0.0, ALU.add, ALU.max)\
                        .then_inc(s["sp_relu"], 1)

            def steps_dt(c, halves=range(HALVES)):
                dve.wait_ge(s["sp_relu"], HALVES * (c + 1))
                for h in halves:
                    dve.wait_ge(s["sp_ready"], HALVES * c + h + 1)
                    V.tensor_tensor(dt[c][:, h, :], sp[c][:, h, :], dt[c][:, h, :], ALU.add).then_inc(s["dt_ready"], 1)

            def steps_dtu(c, halves=range(HALVES)):
                dve.wait_ge(s["u_ready"], HALVES * (c + 1))
                for h in halves:
                    dve.wait_ge(s["dt_ready"], HALVES * c + h + 1)
                    V.tensor_tensor(dtu[c][:, h, :], dt[c][:, h, :], u[c][:, h, :], ALU.mult).then_inc(s["dtu_ready"], 1)

            def drive_early():
                dve.wait_ge(s["dtu_ready"], HALVES)
                dve.wait_ge(s["b_copied"], EARLY + 1)
                V.tensor_tensor(drive[:, EARLY % RD, :, :], dtu[0][:, :, :],
                                b_bc[:, EARLY % RB, :].unsqueeze(1).broadcast_to([P, HALVES, CT]), ALU.mult)\
                    .then_inc(s["drive_early"], 1)

            def scan(i):
                dve.wait_ge(s["decay_ready"], HALVES * (i + 1))
                if i == EARLY:
                    dve.wait_ge(s["drive_early"], 1)
                else:
                    dve.wait_ge(s["drive_ready"], drives(i))
                if i >= RH:
                    dve.wait_ge(s["hc_ready"], i - RH + 1)
                    if shared_step(i - RH):
                        dve.wait_ge(s["hc_side"], sides(i - RH))
                V.tensor_tensor_scan(state[:, i % RH, :, :].rearrange("p h t -> p (h t)"),
                                     decay[:, i % RD, :, :].rearrange("p h t -> p (h t)"),
                                     drive[:, i % RD, :, :].rearrange("p h t -> p (h t)"),
                                     0.0, ALU.mult, ALU.add).then_inc(s["scan_done"], 1)

            def weigh_last(i):
                dve.wait_ge(s["scan_done"], i + 1)
                dve.wait_ge(s["c_mm"], i + 1)
                dve.wait_ge(s["y_mm"], i - RC + 1)
                for h in range(HALVES):
                    V.tensor_tensor(hc[:, i % RC, h, :], state[:, i % RH, h, :], c_ps[i % 2][:, :], ALU.mult)\
                        .then_inc(s["hc_ready"], 1)

            def weigh(i):
                dve.wait_ge(s["scan_done"], i + 1)
                dve.wait_ge(s["c_mm"], i + 1)
                if i >= RC:
                    dve.wait_ge(s["y_mm"], i - RC + 1)
                if shared_step(i):
                    dve.wait_ge(s["c_copied"], sides(i))
                    V.tensor_tensor(hc[:, i % RC, 0, :], state[:, i % RH, 0, :], c_bc[:, :], ALU.mult)\
                        .then_inc(s["hc_ready"], 1)
                    return
                V.tensor_tensor(hc[:, i % RC, :, :], state[:, i % RH, :, :],
                                c_ps[i % 2][:, :].unsqueeze(1).broadcast_to([P, HALVES, CT]), ALU.mult)\
                    .then_inc(s["hc_ready"], 1)

            def gate_z(c):
                dve.wait_ge(s["z_ready"], HALVES * (c + 1))
                for h in range(HALVES):
                    dve.wait_ge(s["y_mm"], N * (c + 1) + (h if c == CHUNKS - 1 else 0))
                    V.tensor_tensor(g[c][:, h, :], y_ps[h][:, :], z_s[c][:, h, :], ALU.mult).then_inc(s["g_ready"], 1)

            def residual(c):
                dve.wait_ge(s["proj_mm"], c + 1)
                dve.wait_ge(s["gate_ready"], 2)
                V.tensor_tensor(x1[c][:, :, :], tiled(att_banks[c]["proj"][:, :]), gate_tok[:, c * TILES:(c + 1) * TILES, :], ALU.mult)\
                    .then_inc(s["gated_ready"], 1)
                if c:
                    dve.wait_ge(s["gated_ready"], c + 1)
                    V.tensor_tensor(x1[c][:, :, :], x1[c][:, :, :], x_sb[:, c * TILES:(c + 1) * TILES, :], ALU.add)\
                        .then_inc(s["x1_ready"], 1)

            def keys(c):
                dve.wait_ge(s["k_mm"], c + 1)
                V.tensor_reduce(k_max[c][:, :], batches(att_banks[c]["k"][:, :]), op=ALU.max, axis=AX.X).then_inc(s["k_max_ready"], 1)
                dve.wait_ge(s["k_max_ready"], c + 1)
                V.tensor_tensor(batches(k_exp[c][:, :]), batches(att_banks[c]["k"][:, :]), over_steps(k_max[c][:, :]), ALU.subtract)\
                    .then_inc(s["k_sub_ready"], 1)

            def queries(c):
                dve.wait_ge(s["q_mm"], c + 1)
                V.tensor_reduce(q_max[c][:, :], in_heads(att_banks[c]["q"][:, :]), op=ALU.max, axis=AX.X).then_inc(s["q_max_ready"], 1)

            def query_shift(c):
                dve.wait_ge(s["q_max_ready"], c + 1)
                V.tensor_tensor(in_heads(q_exp[c][:, :]), in_heads(att_banks[c]["q"][:, :]), over_head(q_max[c][:, :]), ALU.subtract)\
                    .then_inc(s["q_sub_ready"], 1)

            def key_sums(c):
                dve.wait_ge(s["k_exp_ready"], c + 1)
                V.tensor_reduce(k_sum[c][:, :], batches(k_exp[c][:, :]), op=ALU.add, axis=AX.X).then_inc(s["k_sum_ready"], 1)
                dve.wait_ge(s["k_sum_ready"], c + 1)
                V.scalar_tensor_tensor(out=k_den[c][:, :], in0=k_max[c][:, :], scalar=MASKED / 2, in1=k_sum[c][:, :],
                                       op0=ALU.is_ge, op1=ALU.mult).then_inc(s["k_den_ready"], 1)
                dve.wait_ge(s["k_den_ready"], c + 1)
                V.reciprocal(k_inv[c][:, :], k_den[c][:, :]).then_inc(s["k_inv_ready"], 1)

            def soft_keys(c):
                dve.wait_ge(s["k_inv_ready"], c + 1)
                V.tensor_tensor(batches(k_soft[c][:, :]), batches(k_exp[c][:, :]), over_steps(k_inv[c][:, :]), ALU.mult)\
                    .then_inc(s["k_soft_ready"], 1)

            def spread_keys(c, js):
                dve.wait_ge(s["k_T"], c + 1)
                dve.wait_ge(s["kv_mm"], TILES * c)
                for j in js:
                    V.tensor_copy(k_big[j * S:(j + 1) * S, :, j, :], tiled(att_banks[c]["kT"][j * S:(j + 1) * S, :]))\
                        .then_inc(s["k_big_ready"], 1)

            def query_sums(c):
                dve.wait_ge(s["q_exp_ready"], c + 1)
                V.tensor_reduce(q_sum[c][:, :], in_heads(q_exp[c][:, :]), op=ALU.add, axis=AX.X)\
                    .then_inc(s["q_sum_ready"], 1)

            def query_inverses(c):
                dve.wait_ge(s["q_sum_ready"], c + 1)
                V.reciprocal(q_inv[c][:, :], q_sum[c][:, :]).then_inc(s["q_inv_ready"], 1)

            def head_blocks(c, tiles):
                if c:
                    dve.wait_ge(s["y1_mm"], c)
                for t in tiles:
                    bank = att_banks[c]["kv"][t]
                    dve.wait_ge(s["kv_mm"], TILES * c + t + 1)
                    V.tensor_tensor(kv[:, t, :, :], tiled(bank[:, :]), heads.unsqueeze(1).broadcast_to([P, TB, D]),
                                    ALU.mult).then_inc(s["kv_ready"], 1)

            def attended(c):
                dve.wait_ge(s["y1_mm"], c + 1)
                dve.wait_ge(s["q_inv_ready"], c + 1)
                V.tensor_tensor(in_heads(y1[c][:, :, :].rearrange("p t e -> p (t e)")), in_heads(att_banks[c]["y1"][:, :]),
                                over_head(q_inv[c][:, :]), ALU.mult).then_inc(s["y1_ready"], 1)

            def film(c):
                mul, add = film_mul[:, mine(c)], film_add[:, mine(c)]

                def steps(ap, b):
                    return ap[:, b].unsqueeze(2).broadcast_to([P, b.stop - b.start, S])

                for count, p, _, tokens, b in parts_of(c):
                    dve.wait_ge(s["hat2_T"], count)
                    V.tensor_tensor(batches(fh[c][:, tokens]), batches(att_banks[c]["yT"][p][:, tokens]), steps(mul, b),
                                    ALU.mult).then_inc(s["fm_ready"], 1)
                if c:
                    for count, p, _, tokens, b in parts_of(c):
                        dve.wait_ge(s["fm_ready"], count)
                        V.tensor_tensor(batches(fh[c][:, tokens]), batches(fh[c][:, tokens]), steps(add, b), ALU.add)\
                            .then_inc(s["fh_ready"], 1)

            def finish(c):
                dve.wait_ge(s["x1b_ready"], c + 1)
                for count, p, tiles, tokens, _ in parts_of(c):
                    dve.wait_ge(s["fo_mm"], count)
                    t = slice(tiles[0], tiles[-1] + 1)
                    V.tensor_tensor(res[c][:, t, :], tiled(att_banks[c]["out"][p][:, tokens]), x1b[c][:, t, :], ALU.add)\
                        .then_inc(s["res_ready"], 1)

            dve.wait_ge(x_in[0], 16)
            norm_stats(0, ln0, 0, x_tile(0))
            normalise(0, ln0, 0, x_tile(0))
            dve.wait_ge(s["ada_mm"], 1)
            V.tensor_tensor(adas[:, :, :], w1[:, 0:3 * B].rearrange("p (m b) -> p m b", b=B),
                            ada("ada_b").unsqueeze(2).broadcast_to([P, 3, B]), ALU.add).then_inc(s["ada_biased"], 1)
            dve.wait_ge(s["ada_biased"], 1)
            V.tensor_scalar(ln_tmp[:, :], adas[:, 1, :], 1.0, ada("ln_b"), ALU.add, ALU.mult).then_inc(s["ln_tmp_ready"], 1)
            V.tensor_scalar(ln_mul[:, :], adas[:, 1, :], 1.0, ada("ln_g"), ALU.add, ALU.mult).then_inc(s["ln_affine"], 1)
            dve.wait_ge(s["ln_tmp_ready"], 1)
            V.tensor_tensor(ln_add[:, :], ln_tmp[:, :], adas[:, 0, :], ALU.add).then_inc(s["ln_affine"], 1)
            dve.wait_ge(s["ln_affine"], 2)
            adaptive(0)
            conv_taps(0)
            dve.wait_ge(x_in[1], 16)
            dve.wait_ge(s["hat0_T"], 1)
            norm_stats(0, ln0, 1, x_tile(1))
            normalise(0, ln0, 1, x_tile(1))
            dve.wait_ge(s["a_exp_ready"], 1)
            V.tensor_scalar(a_neg[:, :], a_exp[:, :], -1.0, None, ALU.mult).then_inc(s["a_ready"], 1)
            relu_dt(0)
            rest_bc(0)
            split_bc(0)
            for h in range(HALVES):
                steps_dt(0, (h,))
                steps_dtu(0, (h,))
            adaptive(1)
            drive_early()

            def film_constants():
                dve.wait_ge(s["film_mm"], 1)
                V.tensor_tensor(films[:, :, :], w1[:, 0:2 * B].rearrange("p (m b) -> p m b", b=B),
                                att("film_b").unsqueeze(2).broadcast_to([P, 2, B]), ALU.add).then_inc(s["film_biased"], 1)
                dve.wait_ge(s["film_biased"], 1)
                V.tensor_scalar(film_mul[:, :], films[:, 0, :], 1.0, att("fnorm_s"), ALU.add, ALU.mult)\
                    .then_inc(s["film_affine"], 1)
                V.tensor_scalar(film_tmp[:, :], films[:, 0, :], 1.0, att("fnorm_b"), ALU.add, ALU.mult)\
                    .then_inc(s["film_affine"], 1)
                dve.wait_ge(s["film_affine"], 2)
                V.tensor_tensor(film_add[:, :], film_tmp[:, :], films[:, 1, :], ALU.add).then_inc(s["film_affine"], 1)

            for i in range(CHUNKS * N):
                c, n = i // N, i % N
                scan(i)
                if i > 0:
                    weigh(i - 1)
                if c == 0 and 3 <= n < 3 + CONV - 1:
                    conv_taps(1, (n - 2,))
                if c == 0 and n == 14:
                    film_constants()
                if c == 0 and n == 11:
                    rest_bc(1)
                    split_bc(1)
                if c == 0 and n == 12:
                    steps_dt(1)
                if c == 0 and n == 13:
                    steps_dtu(1, (1,))
                if c == 1 and n == 1:
                    gate_z(0)
                if c == 1 and n == 3:
                    residual(0)
                if c == 1 and n == 4:
                    norm_stats(1, ln1, 0, lambda t: x1[0][:, t, :])
                if c == 1 and n == 5:
                    normalise(1, ln1, 0, lambda t: x1[0][:, t, :])
                if c == 1 and n == 8:
                    keys(0)
                if c == 1 and n == 9:
                    queries(0)
                    query_shift(0)
                    key_sums(0)
                if c == 1 and n == 10:
                    query_sums(0)
                    query_inverses(0)
                if c == 1 and n == 12:
                    head_blocks(0, (0, 1, 2))
                if c == 1 and n == 13:
                    head_blocks(0, (3,))
                if c == 1 and n == 14:
                    attended(0)
                    norm_stats(2, ln2, 0, lambda t: y1[0][:, t, :])
            weigh_last(CHUNKS * N - 1)
            normalise(2, ln2, 0, lambda t: y1[0][:, t, :])
            gate_z(1)
            residual(1)
            norm_stats(1, ln1, 1, lambda t: x1[1][:, t, :])
            film(0)
            normalise(1, ln1, 1, lambda t: x1[1][:, t, :])
            keys(1)
            queries(1)
            key_sums(1)
            soft_keys(1)
            query_shift(1)
            spread_keys(1, range(TB // 2, TB))
            query_sums(1)
            query_inverses(1)
            head_blocks(1, range(TILES))
            attended(1)
            norm_stats(2, ln2, 1, lambda t: y1[1][:, t, :])
            finish(0)
            normalise(2, ln2, 1, lambda t: y1[1][:, t, :])
            film(1)
            finish(1)

        @block.tensor
        def _(pe):
            mm = nc.tensor.matmul

            def turn(bank, src, done, ready=None, before=0, tiles=range(TILES)):
                for t in tiles:
                    if ready is not None:
                        pe.wait_ge(ready, before + t + 1)
                    last = nc.tensor.transpose(bank[:, t * P:(t + 1) * P], src(t), ident)
                last.then_inc(done, 1)

            def in_proj(c):
                if c:
                    pe.wait_ge(s["bc_rest_ready"], c)
                turn(w0, lambda t: ln0["hat"][c][:, t, :], s["hat0_T"], s["hat0"], TILES * c)

            def in_proj_x(c):
                pe.wait_ge(s["xn_ready"], c + 1)
                if c:
                    pe.wait_ge(s["sp_relu"], HALVES * c)
                for h, bank in enumerate((w1, w2)):
                    mm(bank[:, :], in_w[:, h, :], xn[c][:, :], start=True, stop=True).then_inc(s["x_mm"], 1)

            def in_proj_z(c, h, bank):
                if c and h:
                    pe.wait_ge(s["conv_tap"], HALVES * (CONV - 1) * (c + 1))
                mm(bank[:, :], in_w[:, HALVES + h, :], xn[c][:, :], start=True, stop=True).then_inc(s["z_mm"], 1)

            def project_dt(c):
                if c:
                    pe.wait_ge(s["z_ready"], HALVES * c + 1)
                for h in range(HALVES):
                    pe.wait_ge(s["u_ready"], HALVES * c + h + 1)
                    last = mm(w0[0:R, :], xp_dt[:, h, :], u[c][:, h, :], start=(h == 0), stop=(h == HALVES - 1))
                last.then_inc(s["dtr_mm"], 1)

            def dt_proj(c):
                pe.wait_ge(s["dtr_ready"], c + 1)
                if c:
                    pe.wait_ge(s["z_ready"], HALVES * (c + 1))
                for h, bank in enumerate((w1, w2)):
                    mm(bank[:, :], dt_w[:, h, :], dt_r[c][:, :], start=True, stop=True).then_inc(s["dt_mm"], 1)

            def project_bc(c, halves=range(HALVES)):
                bank = bc_banks[c]
                if c == 0:
                    pe.wait_ge(s["gate_ready"], 1)
                for h in halves:
                    last = mm(bank[0:PARTS * BCR, :], xp_bc[:, h, :], u[c][:, h, :], start=(h == 0), stop=(h == HALVES - 1))
                if h == HALVES - 1:
                    last.then_inc(s["bc_mm"], 1)

            def spread_b(i):
                c, n = i // N, i % N
                if n == 0:
                    pe.wait_ge(s["bc_ready"], c + 1)
                if i == 0:
                    pe.wait_ge(s["const_gp"], 1)
                if i >= 1:
                    pe.wait_ge(s["b_copied"], i)
                mm(b_ps[:, :], sel[:, n, :], bc_parts[c][:, :], start=True, stop=True).then_inc(s["b_mm"], 1)

            def spread_c(i):
                c, n = i // N, i % N
                if i >= 2:
                    pe.wait_ge(s["hc_ready"], i - 1)
                mm(c_ps[i % 2][:, :], sel[:, N + n, :], bc_parts[c][:, :], start=True, stop=True).then_inc(s["c_mm"], 1)

            def skip_term(c):
                pe.wait_ge(s["const_gp"], 1 + HALVES)
                if c:
                    pe.wait_ge(s["g_ready"], HALVES * c)
                else:
                    pe.wait_ge(s["z_ready"], HALVES)
                for h in range(HALVES):
                    mm(y_ps[h][:, :], diag_d[:, h, :], u[c][:, h, :], start=True, stop=False)

            def sum_states(i):
                n = i % N
                pe.wait_ge(s["hc_ready"], i + 1)
                if shared_step(i):
                    pe.wait_ge(s["hc_side"], sides(i))
                for h in range(HALVES):
                    last = mm(y_ps[h][:, :], ident, hc[:, i % RC, h, :], start=False, stop=(n == N - 1))
                last.then_inc(s["y_mm"], 1)

            def sum_last(i):
                for h in range(HALVES):
                    pe.wait_ge(s["hc_ready"], i + 1 + h)
                    mm(y_ps[h][:, :], ident, hc[:, i % RC, h, :], start=False, stop=True).then_inc(s["y_mm"], 1)

            def out_proj(c):
                if c == 0:
                    pe.wait_ge(s["bc_rest_ready"], CHUNKS)
                    pe.wait_ge(att_in, 16)
                else:
                    pe.wait_ge(s["y1_ready"], c)
                for h in range(HALVES):
                    pe.wait_ge(s["g_ready"], HALVES * c + h + 1)
                    for t in range(TILES):
                        last = mm(att_banks[c]["proj"][:, t * D:(t + 1) * D], g[c][:, h, t * P:(t + 1) * P], out_w[:, h, :],
                                  start=(h == 0 and t == 0), stop=(h == HALVES - 1 and t == TILES - 1))
                last.then_inc(s["proj_mm"], 1)

            def turn_x1(c):
                if c == 0:
                    pe.wait_ge(s["film_biased"], 1)
                else:
                    pe.wait_ge(s["kv_ready"], TILES * c)
                for _, p, tiles, _, _ in parts_of(c):
                    turn(att_banks[c]["x1T"][p], lambda t: ln1["hat"][c][:, t, :], s["hat1_T"], s["hat1"], TILES * c, tiles)

            def bias_first(c, bank, bias):
                mm(bank[:, :], ones_row, bias.unsqueeze(1).broadcast_to([1, TILES, D]), start=True, stop=False)

            def key_bias(c):
                pe.wait_ge(row_in, 48)
                pe.wait_ge(s["mask_ready"], 2)
                mm(att_banks[c]["k"][:, :], key_lhs[:, :], key_rhs[:, c * CT:(c + 1) * CT], start=True, stop=False)

            def key_proj(c):
                for count, p, _, tokens, _ in parts_of(c):
                    pe.wait_ge(s["x1n_ready"], count)
                    last = mm(att_banks[c]["k"][:, tokens], att("wk"), x1n[c][:, tokens], start=False,
                              stop=(p == len(tile_parts[c]) - 1))
                last.then_inc(s["k_mm"], 1)

            def token_proj(c, bank, weight, done):
                for t in range(TILES):
                    last = mm(bank[:, t * D:(t + 1) * D], x1n[c][:, t * P:(t + 1) * P], att(weight),
                              start=False, stop=(t == TILES - 1))
                last.then_inc(done, 1)

            def query_bias(c):
                if c == 0:
                    pe.wait_ge(s["gated_ready"], 1)
                bias_first(c, att_banks[c]["q"], bq_row)

            def value_bias(c):
                if c:
                    pe.wait_ge(s["b_copied"], CHUNKS * N)
                bias_first(c, att_banks[c]["v"], bv_row)

            def turn_q(c):
                pe.wait_ge(s["q_exp_ready"], c + 1)
                if c:
                    pe.wait_ge(s["gated_ready"], c + 1)
                turn(att_banks[c]["qT"], lambda t: q_exp[c][:, t * P:(t + 1) * P], s["q_T"])

            def turn_k(c):
                pe.wait_ge(s["k_soft_ready"], c + 1)
                turn(att_banks[c]["kT"], lambda t: k_soft[c][:, t * P:(t + 1) * P], s["k_T"])

            def key_values(c, tiles):
                pe.wait_ge(s["v_ready"], TILES * (c + 1))
                pe.wait_ge(s["k_big_ready"], TB * (c + 1))
                if c == 0:
                    pe.wait_ge(s["q_cm_ready"], 1)
                for t in tiles:
                    if t == 3 and c == 0:
                        pe.wait_ge(s["kv_ready"], 1)
                    mm(att_banks[c]["kv"][t][:, :], v_sb[c][:, t, :], k_big[:, t, :, :].rearrange("p j e -> p (j e)"),
                       start=True, stop=True).then_inc(s["kv_mm"], 1)

            def attend(c):
                pe.wait_ge(s["q_cm_ready"], c + 1)
                for t in range(TILES):
                    pe.wait_ge(s["kv_ready"], TILES * c + max(t + 1, 2))
                    for j in range(TB):
                        last = mm(att_banks[c]["y1"][j * S:(j + 1) * S, t * D:(t + 1) * D],
                                  q_cm[c][:, (t * TB + j) * S:(t * TB + j + 1) * S], kv[:, t, j, :],
                                  start=True, stop=True, tile_position=(0, j * S))
                last.then_inc(s["y1_mm"], 1)

            def turn_y(c):
                if c:
                    pe.wait_ge(s["v_ready"], TILES * (c + 1))
                for _, p, tiles, _, _ in parts_of(c):
                    turn(att_banks[c]["yT"][p], lambda t: ln2["hat"][c][:, t, :], s["hat2_T"], s["hat2"], TILES * c, tiles)

            def film_out(c):
                for count, p, tiles, _, _ in parts_of(c):
                    pe.wait_ge(s["fs_ready"], count)
                    for t in tiles:
                        last = mm(att_banks[c]["out"][p][:, t * D:(t + 1) * D], fh[c][:, t * P:(t + 1) * P], att("fo_w"),
                                  start=True, stop=True)
                    last.then_inc(s["fo_mm"], 1)

            def film_factors():
                pe.wait_ge(att_in, 16)
                pe.wait_ge(s["sp_relu"], HALVES * CHUNKS)
                for m in range(2):
                    for k in range(KC):
                        last = mm(w1[:, m * B:(m + 1) * B], film_w[:, k, m * D:(m + 1) * D], cond_s[:, k, :],
                                  start=(k == 0), stop=(k == KC - 1))
                last.then_inc(s["film_mm"], 1)

            def turn_gate():
                pe.wait_ge(s["gate_spread"], 1)
                for c in range(CHUNKS):
                    turn(c_ps[c], lambda t: gate_x[:, c * CT + t * P:c * CT + (t + 1) * P], s["gate_mm"])

            def keep_warm(bank, count):
                for _ in range(count):
                    mm(bank[:, 0:P], warm_in[:, :], warm_in[:, :], start=True, stop=True)

            pe.wait_ge(s["cleared"], 1)
            keep_warm(b_ps, 11)
            pe.wait_ge(ada_in, 16)
            pe.wait_ge(s["cond_ready"], 1)
            for m in range(3):
                for k in range(KC):
                    last = mm(w1[:, m * B:(m + 1) * B], ada_w[:, k, m * D:(m + 1) * D], cond_s[:, k, :],
                              start=(k == 0), stop=(k == KC - 1))
            last.then_inc(s["ada_mm"], 1)
            pe.wait_ge(ssm_in, 16)
            in_proj(0)
            keep_warm(b_ps, 4)
            pe.wait_ge(s["ada_biased"], 1)
            in_proj_x(0)
            in_proj_z(0, 0, y_ps[0])
            in_proj_z(0, 1, y_ps[1])
            turn_gate()
            keep_warm(b_ps, 6)
            project_dt(0)
            project_bc(0, (0,))
            dt_proj(0)
            project_bc(0, (1,))
            keep_warm(b_ps, 6)
            in_proj(1)
            keep_warm(b_ps, 2)
            pe.wait_ge(s["gate_ready"], CHUNKS)
            for i in range(RB):
                spread_b(i)
                keep_warm(c_ps[0], 3)
            spread_c(0)
            for i in range(CHUNKS * N):
                c, n = i // N, i % N
                if i + 1 < CHUNKS * N:
                    spread_c(i + 1)
                if c == 0 and n == 1:
                    in_proj_x(1)
                if c == 0 and n == 2:
                    in_proj_z(1, 0, w0)
                if c == 0 and n == 6:
                    in_proj_z(1, 1, w1)
                if c == 0 and n == 7:
                    project_dt(1)
                if c == 0 and n == 8:
                    dt_proj(1)
                if c == 0 and n == 9:
                    project_bc(1)
                if c == 0 and n == 10:
                    film_factors()
                if c == 1 and n == 1:
                    out_proj(0)
                if c == 1 and n == 5:
                    turn_x1(0)
                if c == 1 and n == 6:
                    key_bias(0)
                    key_proj(0)
                if c == 1 and n == 7:
                    query_bias(0)
                    token_proj(0, w0, "wq", s["q_mm"])
                if c == 1 and n == 8:
                    value_bias(0)
                    token_proj(0, w1, "wv", s["v_mm"])
                if c == 1 and n == 10:
                    turn_q(0)
                    turn_k(0)
                if c == 1 and n == 11:
                    key_values(0, (0, 1, 2))
                if c == 1 and n == 12:
                    key_values(0, (3,))
                if c == 1 and n == 13:
                    attend(0)
                if n == 0:
                    if c:
                        sum_states(i - 1)
                    skip_term(c)
                else:
                    sum_states(i - 1)
                if i + RB < CHUNKS * N:
                    spread_b(i + RB)
            sum_last(CHUNKS * N - 1)
            out_proj(1)
            turn_y(0)
            key_bias(1)
            query_bias(1)
            value_bias(1)
            keep_warm(y_ps[1], 5)
            turn_x1(1)
            keep_warm(y_ps[1], 1)
            key_proj(1)
            token_proj(1, c_ps[1], "wq", s["q_mm"])
            token_proj(1, b_ps, "wv", s["v_mm"])
            keep_warm(y_ps[1], 8)
            turn_k(1)
            keep_warm(y_ps[1], 5)
            key_values(1, (0, 1))
            turn_q(1)
            key_values(1, (2, 3))
            attend(1)
            film_out(0)
            keep_warm(w0, 7)
            turn_y(1)
            keep_warm(w0, 6)
            film_out(1)


def kernel(**inputs):
    import numpy as np
    import concourse.bacc as bacc
    from concourse.bass_utils import run_bass_kernel_spmd

    w = {name: np.ascontiguousarray(a) for name, a in inputs.items()}

    def slices(a):
        return np.ascontiguousarray(a.reshape(-1, P, a.shape[-1]).transpose(1, 0, 2)).reshape(P, -1)

    def column(a):
        return slices(a.reshape(-1, 1))

    def high(a):
        return np.concatenate([a, np.zeros((P - a.shape[0], a.shape[1]), a.dtype)])

    eye = np.eye(P, dtype=np.float32)
    xp = w["L0_cond_x_proj_w"].T
    parts = {
        "cond": slices(w["cond_2048"].T), "ada_w": slices(w["L0_cond_ada_w"].T), "ada_b": column(w["L0_cond_ada_b"]),
        "ln_g": column(w["L0_cond_ln_g"]), "ln_b": column(w["L0_cond_ln_b"]),
        "ident": eye, "in_w": w["L0_cond_in_proj_w"].T, "conv_w": slices(w["L0_cond_conv_w"]),
        "conv_b": column(w["L0_cond_conv_b"]), "xp_dt": slices(xp[:, :R]),
        "xp_bc": slices(np.concatenate([xp[:, R:]] * PARTS, axis=1)), "dt_w": high(w["L0_cond_dt_proj_w"].T),
        "dt_b": column(w["L0_cond_dt_proj_b"]), "a_log": slices(w["L0_cond_A_log"]),
        "d_skip": column(w["L0_cond_D_param"]),
        "sel_seed": high(np.concatenate([np.eye(BCR, dtype=np.float32)] * PARTS)),
        "out_w": slices(w["L0_cond_out_proj_w"].T), "norm_s": column(w["L1_cond_norm_scale"]),
        "norm_b": column(w["L1_cond_norm_bias"]), "wq": w["L1_cond_Wq"], "wk": w["L1_cond_Wk"], "wv": w["L1_cond_Wv"],
        "film_w": slices(w["L1_cond_film_emb_W"]), "film_b": column(w["L1_cond_film_emb_b"]),
        "fnorm_s": column(w["L1_cond_film_norm_scale"]), "fnorm_b": column(w["L1_cond_film_norm_bias"]),
        "fo_w": w["L1_cond_film_out_W"],
        "heads": np.kron(np.eye(D // HEAD, dtype=np.float32), np.ones((HEAD, HEAD), np.float32)),
    }

    def pack(names):
        return np.ascontiguousarray(np.concatenate([parts[name] for name, _ in names], axis=1))

    ones = np.ones((1, D), np.float32)
    mask = w["mask_BxS_ik0"]
    feeds = {
        "x": w["x"].reshape(B * S, D), "pack_ada": pack(PACK_ADA), "pack_ssm": pack(PACK_SSM), "pack_att": pack(PACK_ATT),
        "rows": np.concatenate([w["L1_cond_bq"][None], w["L1_cond_bv"][None], ones], axis=1),
        "key_rows": np.concatenate([ones, w["L1_cond_bk"][None]]),
        "mask_row": mask.reshape(1, B * S), "mask_tok": np.ascontiguousarray(mask.reshape(-1, P).T),
        "film_ob": w["L1_cond_film_out_b"],
    }
    nc = bacc.Bacc("TRN2", target_bir_lowering=False, num_devices=1)
    args = [nc.dram_tensor(f"in_{n}_dram", a.shape, mybir.dt.from_np(a.dtype), kind="ExternalInput").ap()
            for n, a in feeds.items()]
    out = nc.dram_tensor("out_0_dram", (B * S, D), mybir.dt.float32, kind="ExternalOutput").ap()
    mamba_attention_kernel(nc, *args, out)
    r = run_bass_kernel_spmd(nc, [{f"in_{n}_dram": a for n, a in feeds.items()}], core_ids=[0])
    return r.results[0]["out_0_dram"].reshape(B, S, D)
```
